# Optimizing a Trainium2 kernel written in Bass

```python
import numpy as np
import jax
import jax.numpy as jnp

def _softmax(x, axis=-1):
    return jax.nn.softmax(x, axis=axis)

def _gelu(x):
    return jax.nn.gelu(x, approximate=True)

def _silu(x):
    return jax.nn.silu(x)

def _sigmoid(x):
    return jax.nn.sigmoid(x)

def _layernorm(x, axis=-1, eps=1e-05):
    m = jnp.mean(x, axis=axis, keepdims=True)
    v = jnp.var(x, axis=axis, keepdims=True)
    return (x - m) / jnp.sqrt(v + eps)

def _scatter_add(tgt, idx, src, axis=0):
    return tgt.at[idx].add(src)

def _segment_sum(src, seg, n):
    return jax.ops.segment_sum(src, seg, n)
kernel_name = 'mk_adj_ffn_d2_adj_r2_a0d0bd'

def setup_inputs(seed: int=0):
    np.random.seed(seed)
    _w = jnp.asarray

    def _rec_inputs():
        import jax
        import jax.numpy as jnp
        _gk = jax.random.key(seed)
        x = -0.0002037 + 1 * jax.random.normal(jax.random.fold_in(_gk, 1), (5000, 128), jnp.float32)
        _w = (1.0 + jnp.arange(5000, dtype=jnp.float32)) ** (-0.5)
        _w = _w / _w.mean()
        _pij = jnp.clip(0.0004 * _w[:, None] * _w[None, :], 0.0, 1.0)
        _a = jax.random.uniform(jax.random.fold_in(_gk, 2), (5000, 5000)) < _pij
        _af = _a.astype(jnp.float32)
        adj = _af
        return (x, adj)
    x, adj = _rec_inputs()

    def _L0_gnn_setup():
        import jax, jax.numpy as jnp
        import numpy as np
        N = 5000
        F = 128
        C = 16
        AL = 0.1
        EPS = 1e-12
        key = jax.random.key(seed)
        k1, k2, k3, k4 = jax.random.split(key, 4)
        A = (jax.random.uniform(k1, (N, N)) > 0.99).astype(jnp.float32)
        x = jax.random.normal(k2, (N, F), dtype=jnp.float32)
        h0 = jax.random.normal(k3, (N, F), dtype=jnp.float32)
        labels = jax.random.randint(k4, (N,), 0, C)
        y = jax.nn.one_hot(labels, C, dtype=jnp.float32)
        return {'input': x, 'A': A, 'h0': h0, 'y': y}
    _L0_gnn_all = _L0_gnn_setup()
    _L0_gnn_in = {k: v for k, v in _L0_gnn_all.items() if k in ('h0', 'y')}
    del _L0_gnn_all

    def _L0_ffn_setup():
        import jax, jax.numpy as jnp
        import numpy as np
        B, S, D, F, E, K = (8, 1024, 128, 512, 8, 2)
        key = jax.random.key(seed)
        ks = jax.random.split(key, 10)
        s = 0.02
        return {'x': jax.random.normal(ks[0], (B, S, D), dtype=jnp.float32), 'Wr': jax.random.normal(ks[1], (D, E), dtype=jnp.float32) * s, 'W1s': jax.random.normal(ks[2], (D, F), dtype=jnp.float32) * s, 'b1s': jnp.zeros((F,), dtype=jnp.float32), 'W2s': jax.random.normal(ks[3], (F, D), dtype=jnp.float32) * s, 'b2s': jnp.zeros((D,), dtype=jnp.float32), 'W1p': jax.random.normal(ks[4], (E, D, F), dtype=jnp.float32) * s, 'b1p': jnp.zeros((E, F), dtype=jnp.float32), 'W2p': jax.random.normal(ks[5], (E, F, D), dtype=jnp.float32) * s, 'b2p': jnp.zeros((E, D), dtype=jnp.float32)}
    _L0_ffn_all = _L0_ffn_setup()
    _L0_ffn_in = {k: v for k, v in _L0_ffn_all.items() if k in ('Wr', 'W1s', 'b1s', 'W2s', 'b2s', 'W1p', 'b1p', 'W2p', 'b2p')}
    del _L0_ffn_all

    def _L1_gnn_setup():
        import jax, jax.numpy as jnp
        import numpy as np
        N = 4096
        D = 128
        OUT = 128
        AVG_DEG = 32
        key = jax.random.key(seed)
        k1, k2, k3, k4, k5 = jax.random.split(key, 5)
        node_features = jax.random.normal(k1, (N, D), dtype=jnp.float32)
        edge_features = jax.random.normal(k2, (N, N), dtype=jnp.float32)
        u = jax.random.uniform(k3, (N, N), dtype=jnp.float32)
        adj = jnp.where(u < AVG_DEG / N, 1.0, 0.0).astype(jnp.float32)
        stdv = 1.0 / np.sqrt(OUT)
        weight = jax.random.uniform(k4, (2 * D + 1, OUT), minval=-stdv, maxval=stdv, dtype=jnp.float32)
        bias = jax.random.uniform(k5, (OUT,), minval=-stdv, maxval=stdv, dtype=jnp.float32)
        return {'node_features': node_features, 'edge_features': edge_features, 'adj': adj, 'weight': weight, 'bias': bias}
    _L1_gnn_all = _L1_gnn_setup()
    _L1_gnn_in = {k: v for k, v in _L1_gnn_all.items() if k in ('weight', 'bias')}
    del _L1_gnn_all

    def _L1_ffn_setup():
        import jax, jax.numpy as jnp
        import numpy as np
        B, T, D, H, E = (16, 2048, 128, 256, 8)
        key = jax.random.key(seed)
        ks = jax.random.split(key, 5)
        x = jax.random.normal(ks[0], (B, T, D), dtype=jnp.float32)
        gate_w = jax.random.normal(ks[1], (D, E), dtype=jnp.float32) * 0.02
        gate_b = jnp.zeros((E,), dtype=jnp.float32)
        W1 = jax.random.normal(ks[2], (E, D, H), dtype=jnp.float32) * 0.02
        b1 = jnp.zeros((E, H), dtype=jnp.float32)
        W2 = jax.random.normal(ks[3], (E, H, D), dtype=jnp.float32) * 0.02
        b2 = jnp.zeros((E, D), dtype=jnp.float32)
        return {'x': x, 'gate_w': gate_w, 'gate_b': gate_b, 'W1': W1, 'b1': b1, 'W2': W2, 'b2': b2}
    _L1_ffn_all = _L1_ffn_setup()
    _L1_ffn_in = {k: v for k, v in _L1_ffn_all.items() if k in ('gate_w', 'gate_b', 'W1', 'b1', 'W2', 'b2')}
    del _L1_ffn_all
    return {'x': x, 'adj': adj, 'L0_gnn_h0': _L0_gnn_in['h0'], 'L0_gnn_y': _L0_gnn_in['y'], 'L0_ffn_Wr': _L0_ffn_in['Wr'], 'L0_ffn_W1s': _L0_ffn_in['W1s'], 'L0_ffn_b1s': _L0_ffn_in['b1s'], 'L0_ffn_W2s': _L0_ffn_in['W2s'], 'L0_ffn_b2s': _L0_ffn_in['b2s'], 'L0_ffn_W1p': _L0_ffn_in['W1p'], 'L0_ffn_b1p': _L0_ffn_in['b1p'], 'L0_ffn_W2p': _L0_ffn_in['W2p'], 'L0_ffn_b2p': _L0_ffn_in['b2p'], 'L1_gnn_weight': _L1_gnn_in['weight'], 'L1_gnn_bias': _L1_gnn_in['bias'], 'L1_ffn_gate_w': _L1_ffn_in['gate_w'], 'L1_ffn_gate_b': _L1_ffn_in['gate_b'], 'L1_ffn_W1': _L1_ffn_in['W1'], 'L1_ffn_b1': _L1_ffn_in['b1'], 'L1_ffn_W2': _L1_ffn_in['W2'], 'L1_ffn_b2': _L1_ffn_in['b2']}

def reference(x, adj, L0_gnn_h0, L0_gnn_y, L0_ffn_Wr, L0_ffn_W1s, L0_ffn_b1s, L0_ffn_W2s, L0_ffn_b2s, L0_ffn_W1p, L0_ffn_b1p, L0_ffn_W2p, L0_ffn_b2p, L1_gnn_weight, L1_gnn_bias, L1_ffn_gate_w, L1_ffn_gate_b, L1_ffn_W1, L1_ffn_b1, L1_ffn_W2, L1_ffn_b2):
    import jax
    import jax.numpy as jnp

    def _L0_gnn_ref(input, A, h0, y):
        import jax, jax.numpy as jnp
        import numpy as np
        N = 5000
        F = 128
        C = 16
        AL = 0.1
        EPS = 1e-12
        adj = A * (y @ y.T)
        row_l1 = jnp.maximum(jnp.sum(jnp.abs(adj), axis=1, keepdims=True), EPS)
        adj = adj / row_l1
        support = adj @ input
        return (1.0 - AL) * support + AL * h0

    def _L0_ffn_ref(x, Wr, W1s, b1s, W2s, b2s, W1p, b1p, W2p, b2p):
        import jax, jax.numpy as jnp
        import numpy as np
        B, S, D, F, E, K = (8, 1024, 128, 512, 8, 2)
        gelu = lambda t: jax.nn.gelu(t, approximate=False)
        shared = gelu(x @ W1s + b1s) @ W2s + b2s
        rw = jax.nn.softmax(x @ Wr, axis=-1)
        topw, topi = jax.lax.top_k(rw, K)
        topw = topw / jnp.sum(topw, axis=-1, keepdims=True)
        mask = jnp.sum(jax.nn.one_hot(topi, E, dtype=topw.dtype) * topw[..., None], axis=-2)
        h = gelu(jnp.einsum('bsd,edf->bsef', x, W1p) + b1p)
        priv = jnp.einsum('bsef,efd->bsed', h, W2p) + b2p
        routed = jnp.einsum('bsed,bse->bsd', priv, mask)
        return shared + routed

    def _L1_gnn_ref(node_features, edge_features, adj, weight, bias):
        import jax, jax.numpy as jnp
        import numpy as np
        N = 4096
        D = 128
        OUT = 128
        AVG_DEG = 32
        neighbor_node_features = adj @ node_features
        neighbor_edge_features = jnp.einsum('ij,ji->i', adj, edge_features)[:, None]
        support = jnp.concatenate((node_features, neighbor_node_features, neighbor_edge_features), axis=1)
        return support @ weight + bias

    def _L1_ffn_ref(x, gate_w, gate_b, W1, b1, W2, b2):
        import jax, jax.numpy as jnp
        import numpy as np
        B, T, D, H, E = (16, 2048, 128, 256, 8)
        Bb, Tt, Dd = x.shape
        Ee = gate_w.shape[1]
        xf = x.reshape(-1, Dd)
        N = xf.shape[0]
        logits = xf @ gate_w + gate_b
        probs = jax.nn.softmax(logits, axis=-1)
        top2_vals, top2_idx = jax.lax.top_k(probs, 2)
        cw = jnp.zeros((N, Ee), dtype=xf.dtype).at[jnp.arange(N)[:, None], top2_idx].add(top2_vals)

        def step(acc, params):
            w1, bb1, w2, bb2, we = params
            h = jax.nn.gelu(xf @ w1 + bb1, approximate=False)
            y = h @ w2 + bb2
            return (acc + we[:, None] * y, None)
        out, _ = jax.lax.scan(step, jnp.zeros_like(xf), (W1, b1, W2, b2, cw.T))
        return out.reshape(Bb, Tt, Dd)
    x = x + _L0_gnn_ref(_layernorm(x, axis=-1), adj, L0_gnn_h0, L0_gnn_y)
    x = x + _L0_ffn_ref(_layernorm(x, axis=-1)[None], L0_ffn_Wr, L0_ffn_W1s, L0_ffn_b1s, L0_ffn_W2s, L0_ffn_b2s, L0_ffn_W1p, L0_ffn_b1p, L0_ffn_W2p, L0_ffn_b2p)[0]
    x = x + _L1_gnn_ref(_layernorm(x, axis=-1), adj, adj, L1_gnn_weight, L1_gnn_bias)
    x = x + _L1_ffn_ref(_layernorm(x, axis=-1)[None], L1_ffn_gate_w, L1_ffn_gate_b, L1_ffn_W1, L1_ffn_b1, L1_ffn_W2, L1_ffn_b2)[0]
    return x

_drawn_inputs = setup_inputs


def setup_inputs(seed=0):
    import zlib

    import numpy as np

    out = dict(_drawn_inputs(seed))
    spreads = {'L0_ffn_b1s': (0.0, 0.1),
     'L0_ffn_b2s': (0.0, 0.1),
     'L0_ffn_b1p': (0.0, 0.406),
     'L0_ffn_b2p': (0.0, 0.1),
     'L1_ffn_gate_b': (0.0, 0.8),
     'L1_ffn_b1': (0.0, 0.8),
     'L1_ffn_b2': (0.0, 0.499)}
    factors = {'L1_ffn_gate_w': 3.81, 'L1_ffn_W1': 8.0, 'L1_ffn_W2': 8.0}
    for name, (base, spread) in spreads.items():
        noise = np.random.default_rng([zlib.crc32(name.encode()), seed]).standard_normal(out[name].shape)
        drawn = base * np.exp(spread * noise) if base else spread * noise
        out[name] = jnp.asarray(drawn.astype(out[name].dtype))
    for name, factor in factors.items():
        out[name] = (out[name] * factor).astype(out[name].dtype)
    return out
```

```python
from contextlib import ExitStack

import numpy as np

import concourse.bass as bass
from concourse import mybir

ALU = mybir.AluOpType
ACT = mybir.ActivationFunctionType
F32 = mybir.dt.float32
F32R = mybir.dt.float32r
BF16 = mybir.dt.bfloat16
AX = mybir.AxisListType

N = 5000
P = 128
D = 128
CW = 512
CH = -(-N // CW)
NB = CH * CW // P
TB = CW // P
CLS = 16
E = 8
ALPHA = 0.1
L1_EPS = 1e-12
LN_EPS = 1e-5
LB = 5
LOADS = NB // LB
LAG = 2
M_BUFS = 4
H_BUFS = 3


class Layer:

    def __init__(self, name, shared, per_expert):
        self.name = name
        self.shared = shared
        self.experts = E + shared
        self.per_expert = per_expert
        self.hidden = self.experts * per_expert
        self.up_step = [h * 36 // self.hidden for h in range(self.hidden)]
        self.add_step = [self.up_step[(e + 1) * per_expert - 1] + LAG + 1 for e in range(self.experts)]

    def down_bank(self, e):
        return e % 2

    def bank_free_count(self, chunk, e):
        same = [x for x in range(e) if self.down_bank(x) == self.down_bank(e)]
        if same:
            return chunk * self.experts + same[-1] + 1
        same = [x for x in range(self.experts) if self.down_bank(x) == self.down_bank(e)]
        return (chunk - 1) * self.experts + same[-1] + 1


def bass_two_layer_gnn_moe_kernel(nc, x_t, adj_in, adj_out, h0_t, y_t, wr0, w1s, b1_0, w2s, b2_0,
                                  w1p, w2p, wg, wg_bias, gate_w, gate_b, w1_1, b1_1, w2_1, b2_1, out):
    ctx = ExitStack()

    def sb(name, shape, dt=F32):
        return ctx.enter_context(nc.sbuf_tensor(name, shape, dt))

    def psum(name):
        return ctx.enter_context(nc.psum_tensor(name, [P, CW], F32))

    def sem(name):
        return ctx.enter_context(nc.semaphore(name))

    LA, LZ = Layer("a", 1, 4), Layer("b", 0, 2)

    xres = sb("xres", [P, NB, D])
    xn = sb("xn", [P, NB, D])
    ysta = sb("ysta", [P, CH * CW], F32R)
    ymov = sb("ymov", [P, CH * CW], F32R)
    w1 = sb("w1", [P, LA.hidden, P])
    w2 = sb("w2", [P, LA.hidden, D])
    b1 = sb("b1", [P, LA.hidden])
    b2 = sb("b2", [P, LA.experts])
    b1z = sb("b1z", [P, LZ.hidden])
    b2z = sb("b2z", [P, LZ.experts])
    ring = sb("ring", [P, 4, LB * CW])
    maskb = sb("maskb", [P, E, CW])
    m = sb("m", [P, M_BUFS, CW])
    h = sb("h", [P, H_BUFS, CW])
    yraw = h[:, 0:2, :]
    wgs = m[:, 0, 0:2 * D].rearrange("p (g o) -> p g o", g=2)
    wedge, wbias, auxf = m[:, 0, 2 * D:3 * D], m[:, 0, 3 * D:4 * D], m[:, 1, :]
    mabs = sb("mabs", [P, 2, CW])
    absum = sb("absum", [P, CW])
    aggf = sb("aggf", [P, CW])
    xnc = sb("xnc", [P, TB, D])
    xnf = sb("xnf", [P, CW])
    ffn = sb("ffn", [P, CW])
    term = sb("term", [P, CW])
    aux = sb("aux", [P, TB, D])
    xnext = sb("xnext", [P, TB, D])
    junk = sb("junk", [P, 2, CW], BF16)
    ident = sb("ident", [P, P])
    ones = sb("ones", [P, 1])
    wr = sb("wr", [P, 2, E])
    gateb = sb("gateb", [P, TB, E])
    stats = sb("stats", [P, NB, 6])
    mv = sb("mv", [P, NB, 2])
    vareps = sb("vareps", [P, NB])
    rstd = sb("rstd", [P, NB])
    mhalf = sb("mhalf", [P, NB])
    redge = sb("redge", [P, NB])
    rpart = sb("rpart", [P, NB])
    rl = sb("rl", [P, TB])
    rinv = sb("rinv", [P, TB])
    lg = sb("lg", [P, TB, E])
    ex = sb("ex", [P, TB, E])
    ex2 = sb("ex2", [P, TB, E])
    rank = sb("rank", [P, TB, E])
    first = sb("first", [P, TB, E])
    second = sb("second", [P, TB, E])
    prio = sb("prio", [P, TB, E])
    mask = sb("mask", [P, TB, E])
    red = sb("red", [P, TB])
    red2 = sb("red2", [P, TB])
    maskt = sb("maskt", [E, CW])

    sbank = [psum("s0"), psum("s1")]
    abank = psum("agg")
    ubank = [psum("u0"), psum("u1")]
    dbank = [psum("d0"), psum("d1")]
    misc = psum("misc")

    mask_dram = nc.dram_tensor("mask_scratch", [2, CH, E, CW], F32, kind="Internal").ap()
    xn_dram = nc.dram_tensor("xn_scratch", [P, NB, D], F32, kind="Internal").ap()

    consts_set = sem("consts_set")
    ident_zeroed = sem("ident_zeroed")
    x_landed = sem("x_landed")
    weights_landed = sem("weights_landed")
    small_landed = sem("small_landed")
    yraw_zeroed = sem("yraw_zeroed")
    yraw_landed = [sem("yraw_landed0"), sem("yraw_landed1")]
    y_step = sem("y_step")
    dve_carried, pool_carried = sem("dve_carried"), sem("pool_carried")
    setup_chain = sem("setup_chain")
    setup_rstd = sem("setup_rstd")
    xn_ready = sem("xn_ready")
    xn_written = sem("xn_written")
    xn_landed = sem("xn_landed")
    xn_last_landed = sem("xn_last_landed")
    weights2_landed = sem("weights2_landed")
    graph_weights_landed = sem("graph_weights_landed")
    ring_landed = [sem(f"ring_landed{i}") for i in range(4)]
    ring2_landed = [sem(f"ring2_landed{i}") for i in range(4)]
    out_written = sem("out_written")
    h0_landed = sem("h0_landed")
    redge_chain = sem("redge_chain")
    edges_read = sem("edges_read")
    s_made = sem("s_made")
    m_made = sem("m_made")
    abs_made = sem("abs_made")
    abs_added = sem("abs_added")
    rowsum_made = sem("rowsum_made")
    rl_chain = sem("rl_chain")
    auxf_made = sem("auxf_made")
    aux_made = sem("aux_made")
    aux_turned = sem("aux_turned")

    NAMES = ["agg_blocks",
             "aggf_made", "agg_turned", "up_made", "gelu_made", "down_made", "experts_added", "term_made",
             "mid_chain", "mid_var", "mid_rstd", "xnc_made", "xnc_turned", "xnf_made", "router_made",
             "lg_made", "router_chain", "exp_made", "mask_chain", "mask_made", "mask_turned", "maskt_made",
             "mask_written", "maskb_landed", "ffn_turned", "end_chain", "end_var", "end_rstd",
             "xnext_made", "xnext_written"]
    SA = {n: sem("a_" + n) for n in NAMES}
    SZ = {n: sem("b_" + n) for n in NAMES}

    def wait(eng, s, value):
        if isinstance(value, int) and value <= 0:
            return
        eng.wait_ge(s, value)

    def carry(eng, s):
        eng.sem_inc(s, 1)

    def cols(chunk):
        return bass.ds(chunk * CW, CW)

    def blks(chunk):
        return bass.ds(chunk * TB, TB)

    def pipeline(eng, iteration):
        for k in range(3):
            iteration(k, True, k >= 1, k >= 2, False)
        with eng.Fori(3, CH) as k:
            iteration(k, True, True, True, True)
        iteration(CH, False, True, True, True)
        iteration(CH + 1, False, False, True, True)
        iteration(CH + 2, False, False, False, True)

    STEPS = NB + LAG + 1
    block = ctx.enter_context(nc.Block())

    @block.sync
    def _(sp):
        for i in range(4):
            sp.dma_start(xres[:, i * 10:(i + 1) * 10, :], x_t[:, i * 10:(i + 1) * 10, :]).then_inc(x_landed, 16)
            sp.wait_ge(x_landed, 16 * (i + 1))

        def a_loads(k):
            for l in range(LOADS):
                slot = l % 2
                wait(sp, edges_read, k * NB + (l - 1) * LB)
                sp.dma_start(ring[:, slot, :], adj_in[k, :, l * LB * CW:(l + 1) * LB * CW]
                             ).then_inc(ring_landed[slot], 16)
                sp.dma_start(ring[:, 2 + slot, :], adj_out[k, :, l * LB * CW:(l + 1) * LB * CW]
                             ).then_inc(ring_landed[2 + slot], 16)

        for l in range(2):
            sp.dma_start(ring[:, l, :], adj_in[0, :, l * LB * CW:(l + 1) * LB * CW]).then_inc(ring_landed[l], 16)
            sp.dma_start(ring[:, 2 + l, :], adj_out[0, :, l * LB * CW:(l + 1) * LB * CW]
                         ).then_inc(ring_landed[2 + l], 16)
        F = LA.per_expert * P
        w1v = w1[:].rearrange("p h q -> p (h q)")
        sp.dma_start(w1v[:, 0:F], w1s).then_inc(weights_landed, 16)
        sp.dma_start(w1v[:, F:].rearrange("p (e f) -> p e f", e=E), w1p.rearrange("e d f -> d e f")
                     ).then_inc(weights_landed, 16)
        sp.dma_start(w2[:, 0:LA.per_expert, :], w2s.rearrange("(k p) d -> p k d", p=P)).then_inc(weights_landed, 16)
        sp.dma_start(w2[:, LA.per_expert:, :], w2p.rearrange("e (k p) d -> p (e k) d", p=P)
                     ).then_inc(weights_landed, 16)
        for l in range(2, LOADS):
            slot = l % 2
            wait(sp, edges_read, (l - 1) * LB)
            sp.dma_start(ring[:, slot, :], adj_in[0, :, l * LB * CW:(l + 1) * LB * CW]
                         ).then_inc(ring_landed[slot], 16)
            sp.dma_start(ring[:, 2 + slot, :], adj_out[0, :, l * LB * CW:(l + 1) * LB * CW]
                         ).then_inc(ring_landed[2 + slot], 16)
        with sp.Fori(1, CH) as k:
            a_loads(k)

        sp.wait_ge(edges_read, CH * NB)
        for l in range(4):
            sp.dma_start(ring[:, l, :], adj_in[0, :, l * LB * CW:(l + 1) * LB * CW]).then_inc(ring2_landed[l], 16)
        sp.wait_ge(SA["agg_blocks"], CH * NB)
        sp.wait_ge(SA["xnext_written"], 16 * (CH - 1))
        sp.dma_start(xn[:, 0:NB - TB, :], xn_dram[:, 0:NB - TB, :]).then_inc(xn_landed, 16)
        sp.wait_ge(abs_made, CH * NB)
        sp.dma_start(wgs, wg[0:2 * D, :].rearrange("(g d) o -> d g o", g=2)).then_inc(graph_weights_landed, 16)
        sp.dma_start(wedge, wg[2 * D:2 * D + 1, :].to_broadcast([P, D])).then_inc(graph_weights_landed, 16)
        sp.dma_start(wbias, wg_bias.to_broadcast([P, D])).then_inc(graph_weights_landed, 16)
        sp.wait_ge(SA["down_made"], CH * LA.hidden)
        sp.dma_start(w1[:, 0:LZ.hidden, :].rearrange("p (e c) q -> p e (c q)", e=E), w1_1.rearrange("e d f -> d e f")
                     ).then_inc(weights2_landed, 16)
        sp.dma_start(w2[:, 0:LZ.hidden, :], w2_1.rearrange("e (k p) d -> p (e k) d", p=P)
                     ).then_inc(weights2_landed, 16)
        sp.wait_ge(SA["xnext_written"], 16 * CH)
        sp.dma_start(xn[:, NB - TB:, :], xn_dram[:, NB - TB:, :]).then_inc(xn_last_landed, 16)

        def z_load(k, l):
            wait(sp, SZ["agg_blocks"], k * NB + (l - 3) * LB)
            sp.dma_start(ring[:, l % 4, :], adj_in[k, :, l * LB * CW:(l + 1) * LB * CW]
                         ).then_inc(ring2_landed[l % 4], 16)

        for l in range(4, LOADS):
            z_load(0, l)
        with sp.Fori(1, CH) as k:
            for l in range(LOADS):
                z_load(k, l)

    @block.tensor
    def _(pe):
        def transposes(src, done):
            for t in range(TB):
                last = pe.transpose(misc[:, t * P:(t + 1) * P], src(t), ident[:])
            last.then_inc(done, 1)

        def up(L, S, j, hb):
            if hb == 0:
                wait(pe, S["xnf_made"], j + 1)
            wait(pe, S["gelu_made"], j * L.hidden + hb - 1)
            pe.matmul(ubank[hb % 2][:], w1[:, hb, :], xnf[:], start=True, stop=True).then_inc(S["up_made"], 1)

        def down(L, S, j, hb):
            e, part = divmod(hb, L.per_expert)
            if part == 0:
                wait(pe, S["experts_added"], L.bank_free_count(j, e))
            wait(pe, S["gelu_made"], j * L.hidden + hb + 1)
            pe.matmul(dbank[L.down_bank(e)][:], w2[:, hb, :], h[:, hb % H_BUFS, :], start=part == 0,
                      stop=part == L.per_expert - 1).then_inc(S["down_made"], 1)

        def hidden_at(L, s):
            return [hb for hb in range(L.hidden) if L.up_step[hb] == s]

        def turn_ffn(L, S, j):
            wait(pe, S["experts_added"], (j + 1) * L.experts)
            transposes(lambda t: ffn[:, t * P:(t + 1) * P], S["ffn_turned"])

        def turn_mask(L, S, j):
            wait(pe, S["mask_made"], j + 1)
            for t in range(TB):
                last = pe.transpose(misc[0:E, t * P:(t + 1) * P], mask[:, t, :], ident[:])
            last.then_inc(S["mask_turned"], 1)

        def turn_norm(L, S, j):
            wait(pe, S["xnc_made"], j + 1)
            transposes(lambda t: xnc[:, t, :], S["xnc_turned"])

        def router(L, S, j, which):
            wait(pe, S["xnf_made"], j + 1)
            for t in range(TB):
                last = pe.matmul(misc[:, t * E:(t + 1) * E], xnf[:, t * P:(t + 1) * P], wr[:, which, :],
                                 start=True, stop=True)
            last.then_inc(S["router_made"], 1)

        def a_iteration(k, agg, mid, run_ffn, end):
            L, S = LA, SA
            for s in range(STEPS):
                if agg and s < NB:
                    if isinstance(k, int) and k == 0 and s % TB == 0:
                        pe.wait_ge(y_step, 5 * (s // TB + 1))
                    wait(pe, m_made, k * NB + s - 1)
                    pe.matmul(sbank[s % 2][:], ysta[:, s * P:(s + 1) * P], ymov[:, cols(k)],
                              start=True, stop=True).then_inc(s_made, 1)
                if run_ffn:
                    for hb in hidden_at(L, s):
                        up(L, S, k - 2, hb)
                if agg and LAG <= s < NB + LAG:
                    b = s - LAG
                    if b == 0:
                        wait(pe, S["aggf_made"], k)
                    wait(pe, m_made, k * NB + b + 1)
                    pe.matmul(abank[:], xn[:, b, :], m[:, b % M_BUFS, :], start=b == 0, stop=b == NB - 1
                              ).then_inc(S["agg_blocks"], 1)
                if run_ffn:
                    for hb in hidden_at(L, s - LAG):
                        down(L, S, k - 2, hb)
                if mid and s == 0:
                    j = k - 1
                    wait(pe, abs_added, k * NB)
                    wait(pe, S["lg_made"], j)
                    for t in range(TB):
                        last = pe.matmul(misc[:, t:t + 1], absum[:, t * P:(t + 1) * P], ones[:],
                                         start=True, stop=True)
                    last.then_inc(rowsum_made, 1)
                if end and s == 1:
                    if mid:
                        wait(pe, rl_chain, 3 * (k - 1) + 1)
                    else:
                        wait(pe, S["lg_made"], k - 1 if run_ffn else k - 2)
                    turn_ffn(L, S, k - 3)
                if run_ffn and s == 3:
                    if end:
                        wait(pe, S["end_chain"], 3 * (k - 3) + 1)
                    wait(pe, rl_chain, 3 * (k - 2) + 1 if not mid else 3 * (k - 1) + 1)
                    turn_mask(L, S, k - 2)
                if mid and s == 5:
                    j = k - 1
                    if run_ffn:
                        wait(pe, S["maskt_made"], k - 1)
                    wait(pe, rl_chain, 3 * j + 1)
                    wait(pe, S["aggf_made"], j + 1)
                    transposes(lambda t: aggf[:, t * P:(t + 1) * P], S["agg_turned"])
                if mid and s == 36:
                    turn_norm(L, S, k - 1)
                if mid and s == 38:
                    router(L, S, k - 1, 0)

        pe.wait_ge(consts_set, 1)
        pe.wait_ge(xn_ready, 2)
        pe.wait_ge(weights_landed, 16 * 4)
        pe.wait_ge(small_landed, 16 * 7)
        pipeline(pe, a_iteration)

        def z_iteration(k, agg, mid, run_ffn, end):
            L, S = LZ, SZ
            for s in range(STEPS):
                if run_ffn:
                    if isinstance(k, int) and k == 2 and s == 0:
                        pe.wait_ge(weights2_landed, 32)
                    for hb in hidden_at(L, s):
                        up(L, S, k - 2, hb)
                if agg and s < NB:
                    b, l = s, s // LB
                    if b == 0:
                        wait(pe, S["aggf_made"], k)
                    if b % LB == 0:
                        wait(pe, ring2_landed[l % 4], 16 * (k * (LOADS // 4) + l // 4 + 1))
                    if isinstance(k, int) and k == 0 and b == NB - TB:
                        pe.wait_ge(xn_last_landed, 16)
                    pe.matmul(abank[:], xn[:, b, :], ring[:, l % 4, (b % LB) * CW:(b % LB + 1) * CW],
                              start=b == 0, stop=b == NB - 1).then_inc(S["agg_blocks"], 1)
                if run_ffn:
                    for hb in hidden_at(L, s - LAG):
                        down(L, S, k - 2, hb)
                if end and s == 1:
                    wait(pe, S["lg_made"], k - 1 if run_ffn else k - 2)
                    turn_ffn(L, S, k - 3)
                if run_ffn and s == 3:
                    wait(pe, S["lg_made"], k - 1)
                    if end:
                        wait(pe, S["xnext_made"], k - 2)
                    turn_mask(L, S, k - 2)
                if mid and s == 5:
                    j = k - 1
                    if run_ffn:
                        wait(pe, S["maskt_made"], k - 1)
                    wait(pe, aux_made, j + 1)
                    transposes(lambda t: aux[:, t, :], aux_turned)
                if mid and s == 8:
                    j = k - 1
                    wait(pe, auxf_made, j + 1)
                    wait(pe, S["aggf_made"], j + 1)
                    if isinstance(k, int) and k == 1:
                        pe.wait_ge(graph_weights_landed, 48)
                    for t in range(TB):
                        pe.matmul(misc[:, t * P:(t + 1) * P], auxf[:, t * P:(t + 1) * P], wgs[:, 0, :],
                                  start=True, stop=False)
                        last = pe.matmul(misc[:, t * P:(t + 1) * P], aggf[:, t * P:(t + 1) * P], wgs[:, 1, :],
                                         start=False, stop=True)
                    last.then_inc(S["agg_turned"], 1)
                if mid and s == 36:
                    turn_norm(L, S, k - 1)
                if mid and s == 38:
                    router(L, S, k - 1, 1)

        pe.wait_ge(xn_landed, 16)
        wait(pe, SA["xnext_made"], CH)
        pipeline(pe, z_iteration)

    @block.scalar
    def _(act):
        def gelu(L, S, j, hb, bias):
            wait(act, S["up_made"], j * L.hidden + hb + 1)
            wait(act, S["down_made"], j * L.hidden + hb + 1 - H_BUFS)
            act.activation(h[:, hb % H_BUFS, :], ubank[hb % 2][:], ACT.Gelu, bias=bias[:, hb:hb + 1]
                           ).then_inc(S["gelu_made"], 1)

        def iteration(L, S, k, agg, mid, run_ffn, bias):
            j = k - 1
            if mid:
                wait(act, S["agg_blocks"], k * NB)
                wait(act, S["agg_turned"], j)
                act.copy(aggf[:], abank[:]).then_inc(S["aggf_made"], 1)
            for s in range(STEPS):
                if run_ffn:
                    for hb in range(L.hidden):
                        if L.up_step[hb] == s:
                            gelu(L, S, k - 2, hb, bias)
                if S is SA and agg and 1 <= s <= NB:
                    b = s - 1
                    wait(act, m_made, k * NB + b + 1)
                    wait(act, abs_added, k * NB + b - 1)
                    act.activation(mabs[:, b % 2, :], m[:, b % M_BUFS, :], ACT.Abs).then_inc(abs_made, 1)
                if run_ffn and s == 2:
                    wait(act, S["mask_turned"], k - 1)
                    wait(act, S["mask_written"], 16 * (k - 2))
                    act.copy(maskt[:], misc[0:E, :]).then_inc(S["maskt_made"], 1)
                if mid and S is SZ and s == 5:
                    wait(act, aux_turned, j + 1)
                    wait(act, S["agg_turned"], j)
                    wait(act, abs_made, CH * NB)
                    act.copy(auxf, misc[:]).then_inc(auxf_made, 1)
                if mid and s == 37:
                    wait(act, S["xnc_turned"], j + 1)
                    if run_ffn:
                        wait(act, S["up_made"], (k - 1) * L.hidden)
                    act.copy(xnf[:], misc[:]).then_inc(S["xnf_made"], 1)
                if mid and s == 41:
                    wait(act, S["lg_made"], j + 1)
                    wait(act, S["mask_made"], j)
                    act.activation(ex[:], lg[:], ACT.Exp).then_inc(S["exp_made"], 1)

        act.wait_ge(small_landed, 16 * 7)
        pipeline(act, lambda k, agg, mid, run_ffn, end: iteration(LA, SA, k, agg, mid, run_ffn, b1))
        pipeline(act, lambda k, agg, mid, run_ffn, end: iteration(LZ, SZ, k, agg, mid, run_ffn, b1z))

    @block.vector
    def _(dve):
        def norm(stat_at, src, dst, chain, base, var_ready, var_count, rstd_ready, rstd_count, n, done, done_inc):
            carry(dve, dve_carried)
            for t in range(n):
                last = dve.bn_stats(stats[:, stat_at + t, :], src(t))
            last.then_inc(chain, 1)
            dve.wait_ge(chain, base + 1)
            carry(dve, dve_carried)
            for t in range(n):
                last = dve.bn_aggr(mv[:, stat_at + t, :], stats[:, stat_at + t, :])
            last.then_inc(chain, 1)
            dve.wait_ge(chain, base + 2)
            dve.tensor_scalar(vareps[:, stat_at:stat_at + n], mv[:, stat_at:stat_at + n, 1], LN_EPS, None, ALU.add
                              ).then_inc(var_ready, 1)
            dve.wait_ge(rstd_ready, rstd_count)
            for t in range(n):
                last = dve.tensor_scalar(dst(t), src(t), mv[:, stat_at + t, 0:1], rstd[:, stat_at + t:stat_at + t + 1],
                                         ALU.subtract, ALU.mult)
            last.then_inc(done, done_inc)

        def router_logits(S, j, biased):
            wait(dve, S["router_made"], j + 1)
            wait(dve, S["exp_made"], j)
            v = misc[:, 0:TB * E].rearrange("p (t e) -> p t e", t=TB)
            if biased:
                dve.tensor_tensor(lg[:], v, gateb[:], ALU.add).then_inc(S["router_chain"], 1)
            else:
                dve.tensor_copy(lg[:], v).then_inc(S["router_chain"], 1)
            wait(dve, S["router_chain"], 2 * j + 1)
            dve.tensor_reduce(red2[:], lg[:], AX.X, ALU.max).then_inc(S["router_chain"], 1)
            wait(dve, S["router_chain"], 2 * j + 2)
            dve.tensor_tensor(lg[:], lg[:], spread(red2), ALU.subtract).then_inc(S["lg_made"], 1)

        def spread(r):
            return r[:].unsqueeze(2).to_broadcast([P, TB, E])

        TOP_STEPS = 15

        def top_two(S, j, over_all):
            count = [0]

            def step(ins):
                count[0] += 1
                ins.then_inc(S["mask_chain"], 1)
                dve.wait_ge(S["mask_chain"], TOP_STEPS * j + count[0])

            def one_hot(dst, src):
                step(dve.tensor_reduce(red[:], src[:], AX.X, ALU.max))
                step(dve.tensor_tensor(rank[:], src[:], spread(red), ALU.is_equal))
                step(dve.tensor_tensor(rank[:], rank[:], prio[:], ALU.mult))
                step(dve.tensor_reduce(red[:], rank[:], AX.X, ALU.max))
                step(dve.tensor_tensor(dst[:], rank[:], spread(red), ALU.is_equal))

            wait(dve, S["exp_made"], j + 1)
            wait(dve, S["mask_turned"], j)
            one_hot(first, ex)
            step(dve.scalar_tensor_tensor(ex2[:], first[:], -2.0, ex[:], ALU.mult, ALU.add))
            one_hot(second, ex2)
            step(dve.tensor_tensor(second[:], first[:], second[:], ALU.add))
            step(dve.tensor_tensor(second[:], second[:], ex[:], ALU.mult))
            step(dve.tensor_reduce(red[:], (ex if over_all else second)[:], AX.X, ALU.add))
            step(dve.reciprocal(red2[:], red[:]))
            assert count[0] == TOP_STEPS
            dve.tensor_tensor(mask[:], second[:], spread(red2), ALU.mult).then_inc(S["mask_made"], 1)

        def add_expert(L, S, j, e, bias):
            wait(dve, S["down_made"], j * L.hidden + (e + 1) * L.per_expert)
            d = dbank[L.down_bank(e)]
            if e == 0:
                wait(dve, S["ffn_turned"], j)
            if e < L.shared:
                dve.tensor_scalar(ffn[:], d[:], bias[:, e:e + 1], None, ALU.add).then_inc(S["experts_added"], 1)
                return
            r = e - L.shared
            if r == 0:
                wait(dve, S["maskb_landed"], 16 * (j + 1))
            if e == 0:
                dve.scalar_tensor_tensor(ffn[:], d[:], bias[:, e:e + 1], maskb[:, r, :], ALU.add, ALU.mult
                                         ).then_inc(S["experts_added"], 1)
                return
            wait(dve, S["experts_added"], j * L.experts + e)
            dve.scalar_tensor_tensor(term[:], d[:], bias[:, e:e + 1], maskb[:, r, :], ALU.add, ALU.mult
                                     ).then_inc(S["term_made"], 1)
            wait(dve, S["term_made"], j * (L.experts - 1) + e)
            dve.tensor_tensor(ffn[:], ffn[:], term[:], ALU.add).then_inc(S["experts_added"], 1)

        for i in range(4):
            dve.wait_ge(x_landed, 16 * (i + 1))
            for b in range(i * 10, i * 10 + 10):
                last = dve.bn_stats(stats[:, b, :], xres[:, b, :])
        last.then_inc(setup_chain, 1)
        dve.wait_ge(setup_chain, 1)
        for b in range(NB):
            last = dve.bn_aggr(mv[:, b, :], stats[:, b, :])
        last.then_inc(setup_chain, 1)
        dve.wait_ge(setup_chain, 2)
        dve.tensor_scalar(vareps[:], mv[:, :, 1], LN_EPS, None, ALU.add).then_inc(setup_chain, 1)
        dve.wait_ge(setup_rstd, 1)
        for b in range(NB):
            last = dve.tensor_scalar(xn[:, b, :], xres[:, b, :], mv[:, b, 0:1], rstd[:, b:b + 1],
                                     ALU.subtract, ALU.mult)
        last.then_inc(xn_ready, 2)
        dve.memset(redge[:], 0.0).then_inc(redge_chain, 1)
        dve.wait_ge(consts_set, 1)
        dve.wait_ge(small_landed, 16 * 7)

        def a_iteration(k, agg, mid, run_ffn, end):
            L, S = LA, SA
            for s in range(STEPS):
                if agg and s < NB:
                    l = s // LB
                    if s % LB == 0:
                        wait(dve, ring_landed[l % 2], 16 * (k * (LOADS // 2) + l // 2 + 1))
                    wait(dve, s_made, k * NB + s + 1)
                    wait(dve, S["agg_blocks"], k * NB + s + 1 - M_BUFS)
                    wait(dve, abs_made, k * NB + s + 1 - M_BUFS)
                    dve.tensor_tensor(m[:, s % M_BUFS, :], sbank[s % 2][:],
                                      ring[:, l % 2, (s % LB) * CW:(s % LB + 1) * CW], ALU.mult).then_inc(m_made, 1)
                if agg and 1 <= s <= NB:
                    b = s - 1
                    l = b // LB
                    piece = slice((b % LB) * CW, (b % LB + 1) * CW)
                    if b % LB == 0:
                        wait(dve, ring_landed[2 + l % 2], 16 * (k * (LOADS // 2) + l // 2 + 1))
                    if b == 0:
                        wait(dve, redge_chain, k + 1)
                    wait(dve, edges_read, k * NB + b - 1)
                    dve.tensor_tensor_reduce(junk[:, b % 2, :], ring[:, l % 2, piece], ring[:, 2 + l % 2, piece],
                                             1.0, 0.0, ALU.mult, ALU.add, rpart[:, b:b + 1]).then_inc(edges_read, 1)
                if agg and LAG <= s < NB + LAG:
                    b = s - LAG
                    wait(dve, abs_made, k * NB + b + 1)
                    if b == 0:
                        wait(dve, rowsum_made, k)
                        dve.tensor_copy(absum[:], mabs[:, b % 2, :]).then_inc(abs_added, 1)
                    else:
                        wait(dve, abs_added, k * NB + b)
                        dve.tensor_tensor(absum[:], mabs[:, b % 2, :], absum[:], ALU.add).then_inc(abs_added, 1)
                if agg and s == NB + 1:
                    wait(dve, edges_read, (k + 1) * NB)
                    wait(dve, redge_chain, k + 1)
                    dve.tensor_tensor(redge[:], redge[:], rpart[:], ALU.add).then_inc(redge_chain, 1)
                if mid and s == 1:
                    j = k - 1
                    wait(dve, rowsum_made, j + 1)
                    dve.tensor_scalar(rl[:], misc[:, 0:TB], L1_EPS, None, ALU.max).then_inc(rl_chain, 1)
                    wait(dve, rl_chain, 3 * j + 1)
                    dve.reciprocal(rinv[:], rl[:]).then_inc(rl_chain, 1)
                    wait(dve, rl_chain, 3 * j + 2)
                    dve.tensor_scalar(rinv[:], rinv[:], 1.0 - ALPHA, None, ALU.mult).then_inc(rl_chain, 1)
                if run_ffn and s == 1:
                    top_two(S, k - 2, False)
                if end and s == 3:
                    j = k - 3
                    wait(dve, S["ffn_turned"], j + 1)
                    dve.tensor_tensor(xres[:, blks(j), :], xres[:, blks(j), :],
                                      misc[:].rearrange("p (t d) -> p t d", t=TB), ALU.add).then_inc(S["end_chain"], 1)
                    wait(dve, S["end_chain"], 3 * j + 1)
                    wait(dve, S["xnext_written"], 16 * j)
                    norm(TB, lambda t: xres[:, bass.ds(j * TB + t, 1), :].rearrange("p o d -> p (o d)"),
                         lambda t: xnext[:, t, :], S["end_chain"], 3 * j + 1, S["end_var"], j + 1, S["end_rstd"], j + 1,
                         TB, S["xnext_made"], 1)
                if mid and s == 7:
                    j = k - 1
                    wait(dve, h0_landed, 16 * (j + 1))
                    dve.scalar_tensor_tensor(xres[:, blks(j), :], aux[:], ALPHA, xres[:, blks(j), :], ALU.mult, ALU.add
                                             ).then_inc(S["mid_chain"], 1)
                    wait(dve, S["mid_chain"], 4 * j + 1)
                    wait(dve, rl_chain, 3 * j + 3)
                    wait(dve, S["agg_turned"], j + 1)
                    for t in range(TB):
                        row = xres[:, bass.ds(j * TB + t, 1), :].rearrange("p o d -> p (o d)")
                        last = dve.scalar_tensor_tensor(row, misc[:, t * P:(t + 1) * P], rinv[:, t:t + 1], row,
                                                        ALU.mult, ALU.add)
                    last.then_inc(S["mid_chain"], 1)
                    wait(dve, S["mid_chain"], 4 * j + 2)
                    wait(dve, S["xnc_turned"], j)
                    norm(0, lambda t: xres[:, bass.ds(j * TB + t, 1), :].rearrange("p o d -> p (o d)"),
                         lambda t: xnc[:, t, :], S["mid_chain"], 4 * j + 2, S["mid_var"], j + 1, S["mid_rstd"], j + 1,
                         TB, S["xnc_made"], 1)
                if run_ffn and s in L.add_step:
                    add_expert(L, S, k - 2, L.add_step.index(s), b2)
                if mid and s == 40:
                    router_logits(S, k - 1, False)

        pipeline(dve, a_iteration)

        def z_iteration(k, agg, mid, run_ffn, end):
            L, S = LZ, SZ
            for s in range(STEPS):
                if run_ffn and s == 1:
                    top_two(S, k - 2, True)
                if end and s == 3:
                    j = k - 3
                    wait(dve, S["ffn_turned"], j + 1)
                    wait(dve, S["xnext_written"], 16 * j)
                    dve.tensor_tensor(xnext[:], xres[:, blks(j), :], misc[:].rearrange("p (t d) -> p t d", t=TB),
                                      ALU.add).then_inc(S["xnext_made"], 1)
                if mid and s == 9:
                    j = k - 1
                    xs = xres[:, blks(j), :]
                    wait(dve, S["agg_turned"], j + 1)
                    dve.tensor_tensor(xs, xs, misc[:].rearrange("p (t d) -> p t d", t=TB), ALU.add
                                      ).then_inc(S["mid_chain"], 1)
                    wait(dve, S["mid_chain"], 5 * j + 1)
                    if isinstance(k, int) and k == 1:
                        dve.wait_ge(graph_weights_landed, 48)
                    dve.tensor_tensor(xs, xs, wbias.unsqueeze(1).to_broadcast([P, TB, D]), ALU.add
                                      ).then_inc(S["mid_chain"], 1)
                    wait(dve, S["mid_chain"], 5 * j + 2)
                    for t in range(TB):
                        row = xres[:, bass.ds(j * TB + t, 1), :].rearrange("p o d -> p (o d)")
                        last = dve.scalar_tensor_tensor(row, wedge, redge[:, bass.ds(j * TB + t, 1)], row,
                                                        ALU.mult, ALU.add)
                    last.then_inc(S["mid_chain"], 1)
                    wait(dve, S["mid_chain"], 5 * j + 3)
                    wait(dve, S["xnc_turned"], j)
                    norm(0, lambda t: xres[:, bass.ds(j * TB + t, 1), :].rearrange("p o d -> p (o d)"),
                         lambda t: xnc[:, t, :], S["mid_chain"], 5 * j + 3, S["mid_var"], j + 1, S["mid_rstd"], j + 1,
                         TB, S["xnc_made"], 1)
                if run_ffn and s in L.add_step:
                    add_expert(L, S, k - 2, L.add_step.index(s), b2z)
                if mid and s == 40:
                    router_logits(S, k - 1, True)

        pipeline(dve, z_iteration)

    @block.gpsimd
    def _(pool):
        pool.memset(mhalf[:], -0.5)
        pool.memset(ones[:], 1.0)
        pool.iota(prio[:], [[0, TB], [-1, E]], base=E, channel_multiplier=0, allow_small_or_imprecise_dtypes=True)
        pool.memset(ident[:], 0.0).then_inc(ident_zeroed, 1)
        pool.memset(yraw, 0.0).then_inc(yraw_zeroed, 1)
        pool.wait_ge(ident_zeroed, 1)
        pool.affine_select(out=ident[:], in_=ident[:], compare_op=ALU.not_equal, fill=1.0, base=0,
                           pattern=[[-1, P]], channel_multiplier=1).then_inc(consts_set, 1)
        pool.wait_ge(yraw_zeroed, 1)

        def load_y(c):
            for g in range(4):
                pool.dma_start(yraw[32 * g:32 * g + CLS, c % 2, :], y_t[:, c * CW:(c + 1) * CW]
                               ).then_inc(yraw_landed[c % 2], 16)

        load_y(0)
        load_y(1)
        pool.dma_start(b1[:], b1_0).then_inc(small_landed, 16)
        pool.dma_start(b2[:], b2_0).then_inc(small_landed, 16)
        pool.dma_start(wr[:, 0, :], wr0).then_inc(small_landed, 16)
        pool.dma_start(wr[:, 1, :], gate_w).then_inc(small_landed, 16)
        pool.dma_start(b1z[:], b1_1).then_inc(small_landed, 16)
        pool.dma_start(b2z[:], b2_1).then_inc(small_landed, 16)
        pool.dma_start(gateb[:], gate_b.to_broadcast([P, TB * E]).rearrange("p (t e) -> p t e", t=TB)
                       ).then_inc(small_landed, 16)

        for c in range(CH):
            pool.wait_ge(yraw_landed[c % 2], 64 * (c // 2 + 1))
            raw, at = yraw[:, c % 2, :], slice(c * CW, (c + 1) * CW)
            pool.tensor_copy(ysta[:, at], raw)
            pool.tensor_copy(ymov[:, at], raw).then_inc(y_step, 1)
            for i, (t, a, b) in enumerate(((ysta, 64, 96), (ysta, 96, 128), (ymov, 32, 64), (ymov, 96, 128))):
                pool.wait_ge(y_step, 5 * c + i + 1)
                pool.tensor_tensor(t[a:b, at], raw[a:b, :], t[a:b, at].bitcast(F32), ALU.subtract
                                   ).then_inc(y_step, 1)
            pool.wait_ge(y_step, 5 * c + 5)
            if c == 0:
                pool.wait_ge(setup_chain, 3)
                pool.tensor_tensor(rstd[:], vareps[:], mhalf[:], ALU.pow).then_inc(setup_rstd, 1)
            if c + 2 < CH:
                load_y(c + 2)

        def power(at, var_ready, done, count):
            wait(pool, var_ready, count)
            pool.tensor_tensor(rstd[:, at:at + TB], vareps[:, at:at + TB], mhalf[:, 0:TB], ALU.pow).then_inc(done, 1)

        def spread_mask(L, S, j, which):
            wait(pool, S["maskt_made"], j + 1)
            carry(pool, pool_carried)
            pool.dma_start(mask_dram[which, bass.ds(j, 1)].rearrange("o e n -> (o e) n"), maskt[:]
                           ).then_inc(S["mask_written"], 16)
            wait(pool, S["mask_written"], 16 * (j + 1))
            wait(pool, S["experts_added"], L.experts * j)
            carry(pool, pool_carried)
            pool.dma_start(maskb[:].rearrange("p e n -> p (e n)"),
                           mask_dram[which, bass.ds(j, 1)].rearrange("o e n -> o (e n)").to_broadcast([P, E * CW])
                           ).then_inc(S["maskb_landed"], 16)

        def a_iteration(k, agg, mid, run_ffn, end):
            if end:
                power(TB, SA["end_var"], SA["end_rstd"], k - 2)
                wait(pool, SA["xnext_made"], k - 2)
                carry(pool, pool_carried)
                pool.dma_start(xn_dram[:, blks(k - 3), :], xnext[:]).then_inc(SA["xnext_written"], 16)
            if run_ffn:
                spread_mask(LA, SA, k - 2, 0)
            if mid:
                power(0, SA["mid_var"], SA["mid_rstd"], k)
            if agg:
                wait(pool, SA["mid_chain"], 4 * (k - 1) + 1)
                carry(pool, pool_carried)
                pool.dma_start(aux[:], h0_t[:, blks(k), :]).then_inc(h0_landed, 16)

        pipeline(pool, a_iteration)

        def z_iteration(k, agg, mid, run_ffn, end):
            if end:
                wait(pool, SZ["xnext_made"], k - 2)
                carry(pool, pool_carried)
                pool.dma_start(out[:, blks(k - 3), :], xnext[:]).then_inc(SZ["xnext_written"], 16)
            if run_ffn:
                spread_mask(LZ, SZ, k - 2, 1)
            if mid:
                if isinstance(k, int) and k == 1:
                    pool.wait_ge(xn_last_landed, 16)
                    pool.wait_ge(xn_landed, 16)
                wait(pool, aux_turned, k - 1)
                pool.tensor_copy(aux[:], xn[:, blks(k - 1), :]).then_inc(aux_made, 1)
                power(0, SZ["mid_var"], SZ["mid_rstd"], k)

        pool.wait_ge(SA["mid_chain"], 4 * CH)
        pipeline(pool, z_iteration)
        pool.wait_ge(SZ["xnext_written"], 16 * CH)

    ctx.close()


def kernel(**inputs):
    import concourse.bacc as _bacc
    from concourse import mybir as _mybir
    from concourse.bass_utils import run_bass_kernel_spmd as _run

    a = {k: np.asarray(v) for k, v in inputs.items()}
    pad = CH * CW

    def rows(v):
        full = np.zeros((pad, v.shape[1]), v.dtype)
        full[:N] = v
        return np.ascontiguousarray(full.reshape(NB, P, -1).transpose(1, 0, 2))

    def columns(v):
        full = np.zeros((pad, pad), v.dtype)
        full[:N, :N] = v
        return np.ascontiguousarray(full.reshape(NB, P, CH, CW).transpose(2, 1, 0, 3).reshape(CH, P, NB * CW))

    y_pad = np.zeros((CLS, pad), a["L0_gnn_y"].dtype)
    y_pad[:, :N] = a["L0_gnn_y"].T

    def per_partition(*parts):
        return np.ascontiguousarray(np.concatenate([v.reshape(-1, P) for v in parts]).T)

    arrays = {
        "x_t": rows(a["x"]),
        "adj_in": columns(a["adj"].T),
        "adj_out": columns(a["adj"]),
        "h0_t": rows(a["L0_gnn_h0"]),
        "y_t": y_pad,
        "wr0": a["L0_ffn_Wr"],
        "w1s": a["L0_ffn_W1s"],
        "b1_0": per_partition(a["L0_ffn_b1s"], a["L0_ffn_b1p"]),
        "w2s": a["L0_ffn_W2s"],
        "b2_0": per_partition(a["L0_ffn_b2s"], a["L0_ffn_b2p"]),
        "w1p": a["L0_ffn_W1p"],
        "w2p": a["L0_ffn_W2p"],
        "wg": a["L1_gnn_weight"],
        "wg_bias": a["L1_gnn_bias"].reshape(1, -1),
        "gate_w": a["L1_ffn_gate_w"],
        "gate_b": np.tile(a["L1_ffn_gate_b"], TB).reshape(1, -1),
        "w1_1": a["L1_ffn_W1"],
        "b1_1": per_partition(a["L1_ffn_b1"]),
        "w2_1": a["L1_ffn_W2"],
        "b2_1": per_partition(a["L1_ffn_b2"]),
    }
    nc = _bacc.Bacc("TRN2", target_bir_lowering=False, num_devices=1, dynamic_dma_scratch_size=8192)
    args, feed = [], {}
    for name, v in arrays.items():
        feed[f"in_{name}"] = np.ascontiguousarray(v)
        args.append(nc.dram_tensor(f"in_{name}", v.shape, _mybir.dt.from_np(v.dtype), kind="ExternalInput").ap())
    args.append(nc.dram_tensor("out_x", [P, NB, D], _mybir.dt.float32, kind="ExternalOutput").ap())
    bass_two_layer_gnn_moe_kernel(nc, *args)
    r = _run(nc, [feed], core_ids=[0])
    got = r.results[0]["out_x"]
    return np.ascontiguousarray(got.transpose(1, 0, 2).reshape(pad, D)[:N])
```

```python
from contextlib import ExitStack

import numpy as np

import concourse.bass as bass
from concourse import mybir

ALU = mybir.AluOpType
ACT = mybir.ActivationFunctionType
F32 = mybir.dt.float32
F32R = mybir.dt.float32r
BF16 = mybir.dt.bfloat16
AX = mybir.AxisListType

N = 5000
P = 128
D = 128
CW = 512
CH = -(-N // CW)
NB = CH * CW // P
TB = CW // P
CLS = 16
E = 8
ALPHA = 0.1
L1_EPS = 1e-12
LN_EPS = 1e-5
LB = 5
LOADS = NB // LB
LAG = 2
M_BUFS = 4
H_BUFS = 3


class Layer:

    def __init__(self, name, shared, per_expert):
        self.name = name
        self.shared = shared
        self.experts = E + shared
        self.per_expert = per_expert
        self.hidden = self.experts * per_expert
        self.up_step = [h * 36 // self.hidden for h in range(self.hidden)]
        self.add_step = [self.up_step[(e + 1) * per_expert - 1] + LAG + 1 for e in range(self.experts)]

    def down_bank(self, e):
        return e % 2

    def bank_free_count(self, chunk, e):
        same = [x for x in range(e) if self.down_bank(x) == self.down_bank(e)]
        if same:
            return chunk * self.experts + same[-1] + 1
        same = [x for x in range(self.experts) if self.down_bank(x) == self.down_bank(e)]
        return (chunk - 1) * self.experts + same[-1] + 1


def bass_two_layer_gnn_moe_kernel(nc, x_t, adj_in, adj_out, h0_t, y_t, wr0, w1s, b1_0, w2s, b2_0,
                                  w1p, w2p, wg, wg_bias, gate_w, gate_b, w1_1, b1_1, w2_1, b2_1, out):
    ctx = ExitStack()

    def sb(name, shape, dt=F32):
        return ctx.enter_context(nc.sbuf_tensor(name, shape, dt))

    def psum(name):
        return ctx.enter_context(nc.psum_tensor(name, [P, CW], F32))

    def sem(name):
        return ctx.enter_context(nc.semaphore(name))

    LA, LZ = Layer("a", 1, 4), Layer("b", 0, 2)

    xres = sb("xres", [P, NB, D])
    xn = sb("xn", [P, NB, D])
    ysta = sb("ysta", [P, CH * CW], F32R)
    ymov = sb("ymov", [P, 2, CW], F32R)
    w1h = sb("w1h", [P, LA.hidden * P], F32R)
    w1l = sb("w1l", [P, LA.hidden * P], F32R)
    w2 = sb("w2", [P, LA.hidden, D])
    b1 = sb("b1", [P, LA.hidden])
    b2 = sb("b2", [P, LA.experts])
    b1z = sb("b1z", [P, LZ.hidden])
    b2z = sb("b2z", [P, LZ.experts])
    ring = sb("ring", [P, 4, LB * CW])
    maskb = sb("maskb", [P, E, CW])
    stage = maskb[:].rearrange("p e n -> p (e n)")
    m = sb("m", [P, M_BUFS, CW])
    h = sb("h", [P, H_BUFS, CW])
    wgs = m[:, 0, 0:2 * D].rearrange("p (g o) -> p g o", g=2)
    wedge, wbias, auxf = m[:, 0, 2 * D:3 * D], m[:, 0, 3 * D:4 * D], m[:, 1, :]
    mabs = sb("mabs", [P, 2, CW])
    absum = sb("absum", [P, CW])
    aggf = sb("aggf", [P, CW])
    xnc = sb("xnc", [P, TB, D])
    xnf = sb("xnf", [P, CW])
    xnfh = sb("xnfh", [P, CW], F32R)
    xnfl = sb("xnfl", [P, CW], F32R)
    YA = E * CW
    hflat = h[:].rearrange("p b n -> p (b n)")
    ffn = sb("ffn", [P, CW])
    term = sb("term", [P, CW])
    aux = sb("aux", [P, TB, D])
    xnext = sb("xnext", [P, TB, D])
    junk = sb("junk", [P, 2, CW], BF16)
    ident = sb("ident", [P, P])
    ones = sb("ones", [P, 1])
    wr = sb("wr", [P, 2, E])
    gateb = sb("gateb", [P, TB, E])
    stats = sb("stats", [P, 2 * TB, 6])
    stats0 = term[:, 0:NB * 6].rearrange("p (b s) -> p b s", b=NB)
    mv = sb("mv", [P, NB, 2])
    vareps = sb("vareps", [P, NB])
    rstd = sb("rstd", [P, NB])
    mhalf = sb("mhalf", [P, NB])
    redge = sb("redge", [P, NB])
    rpart = sb("rpart", [P, NB])
    rl = sb("rl", [P, TB])
    rinv = sb("rinv", [P, TB])
    lg = sb("lg", [P, TB, E])
    ex = sb("ex", [P, TB, E])
    ex2 = sb("ex2", [P, TB, E])
    rank = sb("rank", [P, TB, E])
    first = sb("first", [P, TB, E])
    second = sb("second", [P, TB, E])
    prio = sb("prio", [P, TB, E])
    mask = sb("mask", [P, TB, E])
    red = sb("red", [P, TB])
    red2 = sb("red2", [P, TB])
    maskt = sb("maskt", [E, CW])

    sbank = [psum("s0"), psum("s1")]
    abank = psum("agg")
    ubank = [psum("u0"), psum("u1")]
    dbank = [psum("d0"), psum("d1")]
    misc = psum("misc")

    mask_dram = nc.dram_tensor("mask_scratch", [2, CH, E, CW], F32, kind="Internal").ap()
    xn_dram = nc.dram_tensor("xn_scratch", [P, NB, D], F32, kind="Internal").ap()

    consts_set = sem("consts_set")
    ident_zeroed = sem("ident_zeroed")
    x_landed = [sem(f"x_landed{i}") for i in range(4)]
    weights_landed = sem("weights_landed")
    up_landed = sem("up_landed")
    up_high = sem("up_high")
    up_split = sem("up_split")
    small_landed = sem("small_landed")
    yraw_zeroed = sem("yraw_zeroed")
    yraw_landed = sem("yraw_landed")
    y_high = sem("y_high")
    y_split = sem("y_split")
    ymov_landed = sem("ymov_landed")
    dve_carried, pool_carried, sp_carried = sem("dve_carried"), sem("pool_carried"), sem("sp_carried")
    setup_chain = sem("setup_chain")
    setup_rstd = sem("setup_rstd")
    xn_ready = sem("xn_ready")
    xn_written = sem("xn_written")
    xn_landed = sem("xn_landed")
    xn_last_landed = sem("xn_last_landed")
    weights2_landed = sem("weights2_landed")
    graph_weights_landed = sem("graph_weights_landed")
    ring_landed = [sem(f"ring_landed{i}") for i in range(4)]
    ring2_landed = [sem(f"ring2_landed{i}") for i in range(4)]
    out_written = sem("out_written")
    h0_landed = sem("h0_landed")
    redge_chain = sem("redge_chain")
    edges_read = sem("edges_read")
    s_made = sem("s_made")
    m_made = sem("m_made")
    abs_made = sem("abs_made")
    abs_added = sem("abs_added")
    rowsum_made = sem("rowsum_made")
    rl_chain = sem("rl_chain")
    auxf_made = sem("auxf_made")
    aux_made = sem("aux_made")
    aux_turned = sem("aux_turned")

    NAMES = ["agg_blocks",
             "aggf_made", "agg_turned", "up_made", "gelu_made", "down_made", "experts_added", "term_made",
             "mid_chain", "mid_var", "mid_rstd", "xnc_made", "xnc_turned", "xnf_made", "xnf_split", "router_made",
             "lg_made", "router_chain", "exp_made", "mask_chain", "mask_made", "mask_turned", "maskt_made",
             "mask_written", "maskb_landed", "ffn_turned", "end_chain", "end_var", "end_rstd",
             "xnext_made", "xnext_written"]
    SA = {n: sem("a_" + n) for n in NAMES}
    SZ = {n: sem("b_" + n) for n in NAMES}

    def wait(eng, s, value):
        if isinstance(value, int) and value <= 0:
            return
        eng.wait_ge(s, value)

    def carry(eng, s):
        eng.sem_inc(s, 1)

    def cols(chunk):
        return bass.ds(chunk * CW, CW)

    def blks(chunk):
        return bass.ds(chunk * TB, TB)

    def pipeline(eng, iteration):
        for k in range(3):
            iteration(k, True, k >= 1, k >= 2, False)
        with eng.Fori(3, CH) as k:
            iteration(k, True, True, True, True)
        iteration(CH, False, True, True, True)
        iteration(CH + 1, False, False, True, True)
        iteration(CH + 2, False, False, False, True)

    STEPS = NB + LAG + 1
    block = ctx.enter_context(nc.Block())

    @block.sync
    def _(sp):
        for i in range(4):
            sp.dma_start(xres[:, i * 10:(i + 1) * 10, :], x_t[:, i * 10:(i + 1) * 10, :]).then_inc(x_landed[i], 16)

        def both_loads(k, l):
            slot, at = l % 2, slice(l * LB * CW, (l + 1) * LB * CW)
            wait(sp, edges_read, k * NB + (l - 1) * LB)
            sp.dma_start(ring[:, slot, :], adj_in[k, :, at]).then_inc(ring_landed[slot], 16)
            sp.dma_start(ring[:, 2 + slot, :], adj_out[k, :, at]).then_inc(ring_landed[2 + slot], 16)

        def load_ymov(k, buf):
            wait(sp, s_made, (k - 1) * NB)
            carry(sp, sp_carried)
            wait(sp, ymov_landed, 64 * k)
            carry(sp, sp_carried)
            for dst, src in enumerate((0, 2, 1, 3)):
                sp.dma_start(ymov[32 * dst:32 * dst + 32, buf, :].bitcast(F32),
                             ysta[32 * src:32 * src + 32, cols(k)].bitcast(F32)
                             ).then_inc(ymov_landed, 16)

        both_loads(0, 0)
        both_loads(0, 1)
        sp.wait_ge(y_split, 1)
        load_ymov(0, 0)
        sp.dma_start(ffn[:], w1s).then_inc(up_landed, 16)
        sp.dma_start(maskb[:], w1p.rearrange("e d f -> d e f")).then_inc(up_landed, 16)
        sp.dma_start(w2[:, 0:LA.per_expert, :], w2s.rearrange("(k p) d -> p k d", p=P)).then_inc(weights_landed, 16)
        sp.dma_start(w2[:, LA.per_expert:, :], w2p.rearrange("e (k p) d -> p (e k) d", p=P)
                     ).then_inc(weights_landed, 16)
        for l in range(2, LOADS):
            both_loads(0, l)
        with sp.Fori(1, CH) as k:
            load_ymov(k, sp.snap(k % 2))
            for l in range(LOADS):
                both_loads(k, l)

        sp.wait_ge(edges_read, CH * NB)
        for l in range(4):
            sp.dma_start(ring[:, l, :], adj_in[0, :, l * LB * CW:(l + 1) * LB * CW]).then_inc(ring2_landed[l], 16)
        sp.wait_ge(SA["agg_blocks"], CH * NB)
        sp.wait_ge(SA["xnext_written"], 16 * (CH - 1))
        sp.dma_start(xn[:, 0:NB - TB, :], xn_dram[:, 0:NB - TB, :]).then_inc(xn_landed, 16)
        sp.wait_ge(abs_made, CH * NB)
        sp.dma_start(wgs, wg[0:2 * D, :].rearrange("(g d) o -> d g o", g=2)).then_inc(graph_weights_landed, 16)
        sp.dma_start(wedge, wg[2 * D:2 * D + 1, :].to_broadcast([P, D])).then_inc(graph_weights_landed, 16)
        sp.dma_start(wbias, wg_bias.to_broadcast([P, D])).then_inc(graph_weights_landed, 16)
        sp.wait_ge(SA["down_made"], CH * LA.hidden)
        sp.dma_start(w2[:, 0:LZ.hidden, :], w2_1.rearrange("e (k p) d -> p (e k) d", p=P)
                     ).then_inc(weights2_landed, 16)
        sp.wait_ge(SA["experts_added"], CH * LA.experts)
        sp.dma_start(stage[:, 0:LZ.hidden * P].rearrange("p (e f) -> p e f", e=E), w1_1.rearrange("e d f -> d e f")
                     ).then_inc(up_landed, 16)
        sp.wait_ge(SA["xnext_written"], 16 * CH)
        sp.dma_start(xn[:, NB - TB:, :], xn_dram[:, NB - TB:, :]).then_inc(xn_last_landed, 16)

        def z_load(k, l):
            wait(sp, SZ["agg_blocks"], k * NB + (l - 3) * LB)
            sp.dma_start(ring[:, l % 4, :], adj_in[k, :, l * LB * CW:(l + 1) * LB * CW]
                         ).then_inc(ring2_landed[l % 4], 16)

        for l in range(4, LOADS):
            z_load(0, l)
        with sp.Fori(1, CH) as k:
            for l in range(LOADS):
                z_load(k, l)

    @block.tensor
    def _(pe):
        def transposes(src, done):
            for t in range(TB):
                last = pe.transpose(misc[:, t * P:(t + 1) * P], src(t), ident[:])
            last.then_inc(done, 1)

        def up(L, S, j, hb):
            if hb == 0:
                wait(pe, S["xnf_split"], j + 1)
            wait(pe, S["gelu_made"], j * L.hidden + hb - 1)
            at, u = slice(hb * P, (hb + 1) * P), ubank[hb % 2]
            pe.matmul(u[:], w1h[:, at], xnfh[:], start=True, stop=False)
            pe.matmul(u[:], w1h[:, at], xnfl[:], start=False, stop=False)
            pe.matmul(u[:], w1l[:, at], xnfh[:], start=False, stop=True).then_inc(S["up_made"], 1)

        def down(L, S, j, hb):
            e, part = divmod(hb, L.per_expert)
            if part == 0:
                wait(pe, S["experts_added"], L.bank_free_count(j, e))
            wait(pe, S["gelu_made"], j * L.hidden + hb + 1)
            pe.matmul(dbank[L.down_bank(e)][:], w2[:, hb, :], h[:, hb % H_BUFS, :], start=part == 0,
                      stop=part == L.per_expert - 1).then_inc(S["down_made"], 1)

        def hidden_at(L, s):
            return [hb for hb in range(L.hidden) if L.up_step[hb] == s]

        def turn_ffn(L, S, j):
            wait(pe, S["experts_added"], (j + 1) * L.experts)
            transposes(lambda t: ffn[:, t * P:(t + 1) * P], S["ffn_turned"])

        def turn_mask(L, S, j):
            wait(pe, S["mask_made"], j + 1)
            for t in range(TB):
                last = pe.transpose(misc[0:E, t * P:(t + 1) * P], mask[:, t, :], ident[:])
            last.then_inc(S["mask_turned"], 1)

        def turn_norm(L, S, j):
            wait(pe, S["xnc_made"], j + 1)
            transposes(lambda t: xnc[:, t, :], S["xnc_turned"])

        def router(L, S, j, which):
            wait(pe, S["xnf_made"], j + 1)
            for t in range(TB):
                last = pe.matmul(misc[:, t * E:(t + 1) * E], xnf[:, t * P:(t + 1) * P], wr[:, which, :],
                                 start=True, stop=True)
            last.then_inc(S["router_made"], 1)

        def a_iteration(k, agg, mid, run_ffn, end):
            L, S = LA, SA
            for s in range(STEPS):
                if agg and s < NB:
                    if s == 0:
                        wait(pe, ymov_landed, 64 * (k + 1))
                    wait(pe, m_made, k * NB + s - 1)
                    pe.matmul(sbank[s % 2][:], ysta[:, s * P:(s + 1) * P], ymov[:, k % 2, :],
                              start=True, stop=True).then_inc(s_made, 1)
                if run_ffn:
                    if isinstance(k, int) and k == 2 and s == 0:
                        pe.wait_ge(up_split, 1)
                        pe.wait_ge(weights_landed, 32)
                    for hb in hidden_at(L, s):
                        up(L, S, k - 2, hb)
                if agg and LAG <= s < NB + LAG:
                    b = s - LAG
                    if b == 0:
                        wait(pe, S["aggf_made"], k)
                    wait(pe, m_made, k * NB + b + 1)
                    pe.matmul(abank[:], xn[:, b, :], m[:, b % M_BUFS, :], start=b == 0, stop=b == NB - 1
                              ).then_inc(S["agg_blocks"], 1)
                if run_ffn:
                    for hb in hidden_at(L, s - LAG):
                        down(L, S, k - 2, hb)
                if mid and s == 0:
                    j = k - 1
                    wait(pe, abs_added, k * (NB - 1))
                    wait(pe, S["lg_made"], j)
                    for t in range(TB):
                        last = pe.matmul(misc[:, t:t + 1], absum[:, t * P:(t + 1) * P], ones[:],
                                         start=True, stop=True)
                    last.then_inc(rowsum_made, 1)
                if end and s == 1:
                    if mid:
                        wait(pe, rl_chain, 3 * (k - 1) + 1)
                    else:
                        wait(pe, S["lg_made"], k - 1 if run_ffn else k - 2)
                    turn_ffn(L, S, k - 3)
                if run_ffn and s == 3:
                    if end:
                        wait(pe, S["end_chain"], 3 * (k - 3) + 1)
                    wait(pe, rl_chain, 3 * (k - 2) + 1 if not mid else 3 * (k - 1) + 1)
                    turn_mask(L, S, k - 2)
                if mid and s == 5:
                    j = k - 1
                    if run_ffn:
                        wait(pe, S["maskt_made"], k - 1)
                    wait(pe, rl_chain, 3 * j + 1)
                    wait(pe, S["aggf_made"], j + 1)
                    transposes(lambda t: aggf[:, t * P:(t + 1) * P], S["agg_turned"])
                if mid and s == 36:
                    turn_norm(L, S, k - 1)
                if mid and s == 38:
                    router(L, S, k - 1, 0)

        pe.wait_ge(consts_set, 1)
        pe.wait_ge(xn_ready, 2)
        pe.wait_ge(y_split, 1)
        pe.wait_ge(small_landed, 16 * 7)
        pipeline(pe, a_iteration)

        def z_iteration(k, agg, mid, run_ffn, end):
            L, S = LZ, SZ
            for s in range(STEPS):
                if run_ffn:
                    if isinstance(k, int) and k == 2 and s == 0:
                        pe.wait_ge(up_split, 2)
                        pe.wait_ge(weights2_landed, 16)
                    for hb in hidden_at(L, s):
                        up(L, S, k - 2, hb)
                if agg and s < NB:
                    b, l = s, s // LB
                    if b == 0:
                        wait(pe, S["aggf_made"], k)
                    if b % LB == 0:
                        wait(pe, ring2_landed[l % 4], 16 * (k * (LOADS // 4) + l // 4 + 1))
                    if isinstance(k, int) and k == 0 and b == NB - TB:
                        pe.wait_ge(xn_last_landed, 16)
                    pe.matmul(abank[:], xn[:, b, :], ring[:, l % 4, (b % LB) * CW:(b % LB + 1) * CW],
                              start=b == 0, stop=b == NB - 1).then_inc(S["agg_blocks"], 1)
                if run_ffn:
                    for hb in hidden_at(L, s - LAG):
                        down(L, S, k - 2, hb)
                if end and s == 1:
                    wait(pe, S["lg_made"], k - 1 if run_ffn else k - 2)
                    turn_ffn(L, S, k - 3)
                if run_ffn and s == 3:
                    wait(pe, S["lg_made"], k - 1)
                    if end:
                        wait(pe, S["xnext_made"], k - 2)
                    turn_mask(L, S, k - 2)
                if mid and s == 5:
                    j = k - 1
                    if run_ffn:
                        wait(pe, S["maskt_made"], k - 1)
                    wait(pe, aux_made, j + 1)
                    transposes(lambda t: aux[:, t, :], aux_turned)
                if mid and s == 8:
                    j = k - 1
                    wait(pe, auxf_made, j + 1)
                    wait(pe, S["aggf_made"], j + 1)
                    if isinstance(k, int) and k == 1:
                        pe.wait_ge(graph_weights_landed, 48)
                    for t in range(TB):
                        pe.matmul(misc[:, t * P:(t + 1) * P], auxf[:, t * P:(t + 1) * P], wgs[:, 0, :],
                                  start=True, stop=False)
                        last = pe.matmul(misc[:, t * P:(t + 1) * P], aggf[:, t * P:(t + 1) * P], wgs[:, 1, :],
                                         start=False, stop=True)
                    last.then_inc(S["agg_turned"], 1)
                if mid and s == 36:
                    turn_norm(L, S, k - 1)
                if mid and s == 38:
                    router(L, S, k - 1, 1)

        pe.wait_ge(xn_landed, 16)
        wait(pe, SA["xnext_made"], CH)
        pipeline(pe, z_iteration)

    @block.scalar
    def _(act):
        def gelu(L, S, j, hb, bias):
            wait(act, S["up_made"], j * L.hidden + hb + 1)
            wait(act, S["down_made"], j * L.hidden + hb + 1 - H_BUFS)
            act.activation(h[:, hb % H_BUFS, :], ubank[hb % 2][:], ACT.Gelu, bias=bias[:, hb:hb + 1]
                           ).then_inc(S["gelu_made"], 1)

        def iteration(L, S, k, agg, mid, run_ffn, bias):
            j = k - 1
            if mid:
                wait(act, S["agg_blocks"], k * NB)
                wait(act, S["agg_turned"], j)
                act.copy(aggf[:], abank[:]).then_inc(S["aggf_made"], 1)
            for s in range(STEPS):
                if run_ffn:
                    for hb in range(L.hidden):
                        if L.up_step[hb] == s:
                            gelu(L, S, k - 2, hb, bias)
                if S is SA and agg and 1 <= s <= NB:
                    b = s - 1
                    wait(act, m_made, k * NB + b + 1)
                    if b == 0:
                        wait(act, rowsum_made, k)
                    else:
                        wait(act, abs_added, k * (NB - 1) + max(b - 2, 0))
                    act.activation(mabs[:, b % 2, :] if b else absum[:], m[:, b % M_BUFS, :], ACT.Abs
                                   ).then_inc(abs_made, 1)
                if run_ffn and s == 2:
                    wait(act, S["mask_turned"], k - 1)
                    wait(act, S["mask_written"], 16 * (k - 2))
                    act.copy(maskt[:], misc[0:E, :]).then_inc(S["maskt_made"], 1)
                if mid and S is SZ and s == 5:
                    wait(act, aux_turned, j + 1)
                    wait(act, S["agg_turned"], j)
                    wait(act, abs_made, CH * NB)
                    act.copy(auxf, misc[:]).then_inc(auxf_made, 1)
                if mid and s == 37:
                    wait(act, S["xnc_turned"], j + 1)
                    if run_ffn:
                        wait(act, S["up_made"], (k - 1) * L.hidden)
                    act.copy(xnfh[:], misc[:])
                    act.copy(xnf[:], misc[:]).then_inc(S["xnf_made"], 1)
                if mid and s == 41:
                    wait(act, S["lg_made"], j + 1)
                    wait(act, S["mask_made"], j)
                    act.activation(ex[:], lg[:], ACT.Exp).then_inc(S["exp_made"], 1)

        act.wait_ge(yraw_zeroed, 1)
        for g in range(4):
            rows = slice(32 * g, 32 * g + CLS)
            act.dma_start(stage[rows, 0:YA], y_t[:, 0:YA]).then_inc(yraw_landed, 16)
            act.dma_start(hflat[rows, 0:CH * CW - YA], y_t[:, YA:]).then_inc(yraw_landed, 16)
        act.wait_ge(yraw_landed, 16 * 8)
        act.copy(ysta[:, 0:YA], stage)
        act.copy(ysta[:, YA:], hflat[:, 0:CH * CW - YA]).then_inc(y_high, 1)
        act.wait_ge(small_landed, 16 * 7)
        act.wait_ge(up_landed, 32)
        F = LA.per_expert * P
        act.copy(w1h[:, 0:F], ffn[:])
        act.copy(w1h[:, F:], stage).then_inc(up_high, 1)
        pipeline(act, lambda k, agg, mid, run_ffn, end: iteration(LA, SA, k, agg, mid, run_ffn, b1))
        act.wait_ge(up_landed, 48)
        act.copy(w1h[:, 0:LZ.hidden * P], stage[:, 0:LZ.hidden * P]).then_inc(up_high, 1)
        pipeline(act, lambda k, agg, mid, run_ffn, end: iteration(LZ, SZ, k, agg, mid, run_ffn, b1z))

    @block.vector
    def _(dve):
        def norm(stat_at, src, dst, chain, base, var_ready, var_count, rstd_ready, rstd_count, n, done, done_inc):
            carry(dve, dve_carried)
            for t in range(n):
                last = dve.bn_stats(stats[:, stat_at + t, :], src(t))
            last.then_inc(chain, 1)
            dve.wait_ge(chain, base + 1)
            carry(dve, dve_carried)
            for t in range(n):
                last = dve.bn_aggr(mv[:, stat_at + t, :], stats[:, stat_at + t, :])
            last.then_inc(chain, 1)
            dve.wait_ge(chain, base + 2)
            dve.tensor_scalar(vareps[:, stat_at:stat_at + n], mv[:, stat_at:stat_at + n, 1], LN_EPS, None, ALU.add
                              ).then_inc(var_ready, 1)
            dve.wait_ge(rstd_ready, rstd_count)
            for t in range(n):
                last = dve.tensor_scalar(dst(t), src(t), mv[:, stat_at + t, 0:1], rstd[:, stat_at + t:stat_at + t + 1],
                                         ALU.subtract, ALU.mult)
            last.then_inc(done, done_inc)

        def norm_low(S, j):
            wait(dve, S["xnf_made"], j + 1)
            split_low(xnfl[:], xnf[:], xnfh[:]).then_inc(S["xnf_split"], 1)

        def router_logits(S, j, biased):
            wait(dve, S["router_made"], j + 1)
            wait(dve, S["exp_made"], j)
            v = misc[:, 0:TB * E].rearrange("p (t e) -> p t e", t=TB)
            if biased:
                dve.tensor_tensor(lg[:], v, gateb[:], ALU.add).then_inc(S["router_chain"], 1)
            else:
                dve.tensor_copy(lg[:], v).then_inc(S["router_chain"], 1)
            wait(dve, S["router_chain"], 2 * j + 1)
            dve.tensor_reduce(red2[:], lg[:], AX.X, ALU.max).then_inc(S["router_chain"], 1)
            wait(dve, S["router_chain"], 2 * j + 2)
            dve.tensor_tensor(lg[:], lg[:], spread(red2), ALU.subtract).then_inc(S["lg_made"], 1)

        def spread(r):
            return r[:].unsqueeze(2).to_broadcast([P, TB, E])

        TOP_STEPS = 15

        def top_two(S, j, over_all):
            count = [0]

            def step(ins):
                count[0] += 1
                ins.then_inc(S["mask_chain"], 1)
                dve.wait_ge(S["mask_chain"], TOP_STEPS * j + count[0])

            def one_hot(dst, src):
                step(dve.tensor_reduce(red[:], src[:], AX.X, ALU.max))
                step(dve.tensor_tensor(rank[:], src[:], spread(red), ALU.is_equal))
                step(dve.tensor_tensor(rank[:], rank[:], prio[:], ALU.mult))
                step(dve.tensor_reduce(red[:], rank[:], AX.X, ALU.max))
                step(dve.tensor_tensor(dst[:], rank[:], spread(red), ALU.is_equal))

            wait(dve, S["exp_made"], j + 1)
            wait(dve, S["mask_turned"], j)
            one_hot(first, ex)
            step(dve.scalar_tensor_tensor(ex2[:], first[:], -2.0, ex[:], ALU.mult, ALU.add))
            one_hot(second, ex2)
            step(dve.tensor_tensor(second[:], first[:], second[:], ALU.add))
            step(dve.tensor_tensor(second[:], second[:], ex[:], ALU.mult))
            step(dve.tensor_reduce(red[:], (ex if over_all else second)[:], AX.X, ALU.add))
            step(dve.reciprocal(red2[:], red[:]))
            assert count[0] == TOP_STEPS
            dve.tensor_tensor(mask[:], second[:], spread(red2), ALU.mult).then_inc(S["mask_made"], 1)

        def add_expert(L, S, j, e, bias):
            wait(dve, S["down_made"], j * L.hidden + (e + 1) * L.per_expert)
            d = dbank[L.down_bank(e)]
            if e == 0:
                wait(dve, S["ffn_turned"], j)
            if e < L.shared:
                dve.tensor_scalar(ffn[:], d[:], bias[:, e:e + 1], None, ALU.add).then_inc(S["experts_added"], 1)
                return
            r = e - L.shared
            if r == 0:
                wait(dve, S["maskb_landed"], 16 * (j + 1))
            if e == 0:
                dve.scalar_tensor_tensor(ffn[:], d[:], bias[:, e:e + 1], maskb[:, r, :], ALU.add, ALU.mult
                                         ).then_inc(S["experts_added"], 1)
                return
            wait(dve, S["experts_added"], j * L.experts + e)
            dve.scalar_tensor_tensor(term[:], d[:], bias[:, e:e + 1], maskb[:, r, :], ALU.add, ALU.mult
                                     ).then_inc(S["term_made"], 1)
            wait(dve, S["term_made"], j * (L.experts - 1) + e)
            dve.tensor_tensor(ffn[:], ffn[:], term[:], ALU.add).then_inc(S["experts_added"], 1)

        def split_low(low, raw, high):
            return dve.tensor_tensor(low, raw, high.bitcast(F32), ALU.subtract)

        dve.memset(stage, 0.0)
        dve.memset(hflat[:, 0:CH * CW - YA], 0.0).then_inc(yraw_zeroed, 1)
        for i in range(4):
            dve.wait_ge(x_landed[i], 16)
            for b in range(i * 10, i * 10 + 10):
                last = dve.bn_stats(stats0[:, b, :], xres[:, b, :])
        last.then_inc(setup_chain, 1)
        dve.wait_ge(setup_chain, 1)
        for b in range(NB):
            last = dve.bn_aggr(mv[:, b, :], stats0[:, b, :])
        last.then_inc(setup_chain, 1)
        dve.wait_ge(setup_chain, 2)
        dve.tensor_scalar(vareps[:], mv[:, :, 1], LN_EPS, None, ALU.add).then_inc(setup_chain, 1)
        dve.wait_ge(y_high, 1)
        low = slice(64, 128)
        split_low(ysta[low, 0:YA], stage[low, :], ysta[low, 0:YA])
        split_low(ysta[low, YA:], hflat[low, 0:CH * CW - YA], ysta[low, YA:]).then_inc(y_split, 1)
        dve.wait_ge(setup_rstd, 1)
        for b in range(NB):
            last = dve.tensor_scalar(xn[:, b, :], xres[:, b, :], mv[:, b, 0:1], rstd[:, b:b + 1],
                                     ALU.subtract, ALU.mult)
        last.then_inc(xn_ready, 2)
        dve.memset(redge[:], 0.0).then_inc(redge_chain, 1)
        dve.wait_ge(up_landed, 32)
        dve.wait_ge(up_high, 1)
        F = LA.per_expert * P
        split_low(w1l[:, 0:F], ffn[:], w1h[:, 0:F])
        split_low(w1l[:, F:], stage, w1h[:, F:]).then_inc(up_split, 1)
        dve.wait_ge(consts_set, 1)
        dve.wait_ge(small_landed, 16 * 7)

        def a_iteration(k, agg, mid, run_ffn, end):
            L, S = LA, SA
            for s in range(STEPS):
                if agg and s < NB:
                    l = s // LB
                    if s % LB == 0:
                        wait(dve, ring_landed[l % 2], 16 * (k * (LOADS // 2) + l // 2 + 1))
                    wait(dve, s_made, k * NB + s + 1)
                    wait(dve, S["agg_blocks"], k * NB + s + 1 - M_BUFS)
                    wait(dve, abs_made, k * NB + s + 1 - M_BUFS)
                    dve.tensor_tensor(m[:, s % M_BUFS, :], sbank[s % 2][:],
                                      ring[:, l % 2, (s % LB) * CW:(s % LB + 1) * CW], ALU.mult).then_inc(m_made, 1)
                if agg and 1 <= s <= NB:
                    b = s - 1
                    l = b // LB
                    piece = slice((b % LB) * CW, (b % LB + 1) * CW)
                    if b % LB == 0:
                        wait(dve, ring_landed[2 + l % 2], 16 * (k * (LOADS // 2) + l // 2 + 1))
                    if b == 0:
                        wait(dve, redge_chain, k + 1)
                    wait(dve, edges_read, k * NB + b - 1)
                    dve.tensor_tensor_reduce(junk[:, b % 2, :], ring[:, l % 2, piece], ring[:, 2 + l % 2, piece],
                                             1.0, 0.0, ALU.mult, ALU.add, rpart[:, b:b + 1]).then_inc(edges_read, 1)
                if agg and s == NB + 1:
                    wait(dve, edges_read, (k + 1) * NB)
                    wait(dve, redge_chain, k + 1)
                    dve.tensor_tensor(redge[:], redge[:], rpart[:], ALU.add).then_inc(redge_chain, 1)
                if mid and s == 1:
                    j = k - 1
                    wait(dve, rowsum_made, j + 1)
                    dve.tensor_scalar(rl[:], misc[:, 0:TB], L1_EPS, None, ALU.max).then_inc(rl_chain, 1)
                    wait(dve, rl_chain, 3 * j + 1)
                    dve.reciprocal(rinv[:], rl[:]).then_inc(rl_chain, 1)
                    wait(dve, rl_chain, 3 * j + 2)
                    dve.tensor_scalar(rinv[:], rinv[:], 1.0 - ALPHA, None, ALU.mult).then_inc(rl_chain, 1)
                if run_ffn and s == 1:
                    top_two(S, k - 2, False)
                if end and s == 3:
                    j = k - 3
                    wait(dve, S["ffn_turned"], j + 1)
                    dve.tensor_tensor(xres[:, blks(j), :], xres[:, blks(j), :],
                                      misc[:].rearrange("p (t d) -> p t d", t=TB), ALU.add).then_inc(S["end_chain"], 1)
                    wait(dve, S["end_chain"], 3 * j + 1)
                    wait(dve, S["xnext_written"], 16 * j)
                    norm(TB, lambda t: xres[:, bass.ds(j * TB + t, 1), :].rearrange("p o d -> p (o d)"),
                         lambda t: xnext[:, t, :], S["end_chain"], 3 * j + 1, S["end_var"], j + 1, S["end_rstd"], j + 1,
                         TB, S["xnext_made"], 1)
                if mid and s == 7:
                    j = k - 1
                    wait(dve, h0_landed, 16 * (j + 1))
                    dve.scalar_tensor_tensor(xres[:, blks(j), :], aux[:], ALPHA, xres[:, blks(j), :], ALU.mult, ALU.add
                                             ).then_inc(S["mid_chain"], 1)
                    wait(dve, S["mid_chain"], 4 * j + 1)
                    wait(dve, rl_chain, 3 * j + 3)
                    wait(dve, S["agg_turned"], j + 1)
                    for t in range(TB):
                        row = xres[:, bass.ds(j * TB + t, 1), :].rearrange("p o d -> p (o d)")
                        last = dve.scalar_tensor_tensor(row, misc[:, t * P:(t + 1) * P], rinv[:, t:t + 1], row,
                                                        ALU.mult, ALU.add)
                    last.then_inc(S["mid_chain"], 1)
                    wait(dve, S["mid_chain"], 4 * j + 2)
                    wait(dve, S["xnc_turned"], j)
                    norm(0, lambda t: xres[:, bass.ds(j * TB + t, 1), :].rearrange("p o d -> p (o d)"),
                         lambda t: xnc[:, t, :], S["mid_chain"], 4 * j + 2, S["mid_var"], j + 1, S["mid_rstd"], j + 1,
                         TB, S["xnc_made"], 1)
                if run_ffn and s in L.add_step:
                    add_expert(L, S, k - 2, L.add_step.index(s), b2)
                if mid and s == 38:
                    norm_low(S, k - 1)
                if mid and s == 40:
                    router_logits(S, k - 1, False)

        pipeline(dve, a_iteration)

        def z_iteration(k, agg, mid, run_ffn, end):
            L, S = LZ, SZ
            for s in range(STEPS):
                if run_ffn and s == 1:
                    top_two(S, k - 2, True)
                if end and s == 3:
                    j = k - 3
                    wait(dve, S["ffn_turned"], j + 1)
                    wait(dve, S["xnext_written"], 16 * j)
                    dve.tensor_tensor(xnext[:], xres[:, blks(j), :], misc[:].rearrange("p (t d) -> p t d", t=TB),
                                      ALU.add).then_inc(S["xnext_made"], 1)
                if mid and s == 9:
                    j = k - 1
                    xs = xres[:, blks(j), :]
                    wait(dve, S["agg_turned"], j + 1)
                    dve.tensor_tensor(xs, xs, misc[:].rearrange("p (t d) -> p t d", t=TB), ALU.add
                                      ).then_inc(S["mid_chain"], 1)
                    wait(dve, S["mid_chain"], 5 * j + 1)
                    if isinstance(k, int) and k == 1:
                        dve.wait_ge(graph_weights_landed, 48)
                    dve.tensor_tensor(xs, xs, wbias.unsqueeze(1).to_broadcast([P, TB, D]), ALU.add
                                      ).then_inc(S["mid_chain"], 1)
                    wait(dve, S["mid_chain"], 5 * j + 2)
                    for t in range(TB):
                        row = xres[:, bass.ds(j * TB + t, 1), :].rearrange("p o d -> p (o d)")
                        last = dve.scalar_tensor_tensor(row, wedge, redge[:, bass.ds(j * TB + t, 1)], row,
                                                        ALU.mult, ALU.add)
                    last.then_inc(S["mid_chain"], 1)
                    wait(dve, S["mid_chain"], 5 * j + 3)
                    wait(dve, S["xnc_turned"], j)
                    norm(0, lambda t: xres[:, bass.ds(j * TB + t, 1), :].rearrange("p o d -> p (o d)"),
                         lambda t: xnc[:, t, :], S["mid_chain"], 5 * j + 3, S["mid_var"], j + 1, S["mid_rstd"], j + 1,
                         TB, S["xnc_made"], 1)
                if run_ffn and s in L.add_step:
                    add_expert(L, S, k - 2, L.add_step.index(s), b2z)
                if mid and s == 38:
                    norm_low(S, k - 1)
                if mid and s == 40:
                    router_logits(S, k - 1, True)

        dve.wait_ge(up_high, 2)
        dve.wait_ge(up_landed, 48)
        split_low(w1l[:, 0:LZ.hidden * P], stage[:, 0:LZ.hidden * P], w1h[:, 0:LZ.hidden * P]).then_inc(up_split, 1)
        pipeline(dve, z_iteration)

    @block.gpsimd
    def _(pool):
        pool.memset(mhalf[:], -0.5)
        pool.memset(ones[:], 1.0)
        pool.iota(prio[:], [[0, TB], [-1, E]], base=E, channel_multiplier=0, allow_small_or_imprecise_dtypes=True)
        pool.memset(ident[:], 0.0).then_inc(ident_zeroed, 1)
        pool.wait_ge(ident_zeroed, 1)
        pool.affine_select(out=ident[:], in_=ident[:], compare_op=ALU.not_equal, fill=1.0, base=0,
                           pattern=[[-1, P]], channel_multiplier=1).then_inc(consts_set, 1)
        pool.dma_start(b1[:], b1_0).then_inc(small_landed, 16)
        pool.dma_start(b2[:], b2_0).then_inc(small_landed, 16)
        pool.dma_start(wr[:, 0, :], wr0).then_inc(small_landed, 16)
        pool.dma_start(wr[:, 1, :], gate_w).then_inc(small_landed, 16)
        pool.dma_start(b1z[:], b1_1).then_inc(small_landed, 16)
        pool.dma_start(b2z[:], b2_1).then_inc(small_landed, 16)
        pool.dma_start(gateb[:], gate_b.to_broadcast([P, TB * E]).rearrange("p (t e) -> p t e", t=TB)
                       ).then_inc(small_landed, 16)

        pool.wait_ge(setup_chain, 3)
        pool.tensor_tensor(rstd[:], vareps[:], mhalf[:], ALU.pow).then_inc(setup_rstd, 1)

        def power(at, var_ready, done, count):
            wait(pool, var_ready, count)
            pool.tensor_tensor(rstd[:, at:at + TB], vareps[:, at:at + TB], mhalf[:, 0:TB], ALU.pow).then_inc(done, 1)

        def write_mask(S, j, which):
            wait(pool, S["maskt_made"], j + 1)
            carry(pool, pool_carried)
            pool.dma_start(mask_dram[which, bass.ds(j, 1)].rearrange("o e n -> (o e) n"), maskt[:]
                           ).then_inc(S["mask_written"], 16)

        def spread_mask(L, S, j, which):
            wait(pool, S["mask_written"], 16 * (j + 1))
            wait(pool, S["experts_added"], L.experts * j)
            carry(pool, pool_carried)
            pool.dma_start(maskb[:].rearrange("p e n -> p (e n)"),
                           mask_dram[which, bass.ds(j, 1)].rearrange("o e n -> o (e n)").to_broadcast([P, E * CW])
                           ).then_inc(S["maskb_landed"], 16)

        def a_iteration(k, agg, mid, run_ffn, end):
            for s in range(STEPS):
                if agg and 3 <= s < NB + 2:
                    b = s - 2
                    wait(pool, abs_made, k * NB + b + 1)
                    wait(pool, abs_added, k * (NB - 1) + b - 1)
                    pool.tensor_tensor(absum[:], mabs[:, b % 2, :], absum[:], ALU.add).then_inc(abs_added, 1)
                if end and s == 3:
                    power(TB, SA["end_var"], SA["end_rstd"], k - 2)
                if run_ffn and s == 4:
                    write_mask(SA, k - 2, 0)
                if end and s == 5:
                    wait(pool, SA["xnext_made"], k - 2)
                    carry(pool, pool_carried)
                    pool.dma_start(xn_dram[:, blks(k - 3), :], xnext[:]).then_inc(SA["xnext_written"], 16)
                if run_ffn and s == 6:
                    spread_mask(LA, SA, k - 2, 0)
                if mid and s == 8:
                    power(0, SA["mid_var"], SA["mid_rstd"], k)
                if agg and s == 10:
                    wait(pool, SA["mid_chain"], 4 * (k - 1) + 1)
                    carry(pool, pool_carried)
                    pool.dma_start(aux[:], h0_t[:, blks(k), :]).then_inc(h0_landed, 16)

        pipeline(pool, a_iteration)

        def z_iteration(k, agg, mid, run_ffn, end):
            if end:
                wait(pool, SZ["xnext_made"], k - 2)
                carry(pool, pool_carried)
                pool.dma_start(out[:, blks(k - 3), :], xnext[:]).then_inc(SZ["xnext_written"], 16)
            if run_ffn:
                write_mask(SZ, k - 2, 1)
                spread_mask(LZ, SZ, k - 2, 1)
            if mid:
                if isinstance(k, int) and k == 1:
                    pool.wait_ge(xn_last_landed, 16)
                    pool.wait_ge(xn_landed, 16)
                wait(pool, aux_turned, k - 1)
                pool.tensor_copy(aux[:], xn[:, blks(k - 1), :]).then_inc(aux_made, 1)
                power(0, SZ["mid_var"], SZ["mid_rstd"], k)

        pool.wait_ge(SA["mid_chain"], 4 * CH)
        pipeline(pool, z_iteration)
        pool.wait_ge(SZ["xnext_written"], 16 * CH)

    ctx.close()


def kernel(**inputs):
    import concourse.bacc as _bacc
    from concourse import mybir as _mybir
    from concourse.bass_utils import run_bass_kernel_spmd as _run

    a = {k: np.asarray(v) for k, v in inputs.items()}
    pad = CH * CW

    def rows(v):
        full = np.zeros((pad, v.shape[1]), v.dtype)
        full[:N] = v
        return np.ascontiguousarray(full.reshape(NB, P, -1).transpose(1, 0, 2))

    def columns(v):
        full = np.zeros((pad, pad), v.dtype)
        full[:N, :N] = v
        return np.ascontiguousarray(full.reshape(NB, P, CH, CW).transpose(2, 1, 0, 3).reshape(CH, P, NB * CW))

    y_pad = np.zeros((CLS, pad), a["L0_gnn_y"].dtype)
    y_pad[:, :N] = a["L0_gnn_y"].T

    def per_partition(*parts):
        return np.ascontiguousarray(np.concatenate([v.reshape(-1, P) for v in parts]).T)

    arrays = {
        "x_t": rows(a["x"]),
        "adj_in": columns(a["adj"].T),
        "adj_out": columns(a["adj"]),
        "h0_t": rows(a["L0_gnn_h0"]),
        "y_t": y_pad,
        "wr0": a["L0_ffn_Wr"],
        "w1s": a["L0_ffn_W1s"],
        "b1_0": per_partition(a["L0_ffn_b1s"], a["L0_ffn_b1p"]),
        "w2s": a["L0_ffn_W2s"],
        "b2_0": per_partition(a["L0_ffn_b2s"], a["L0_ffn_b2p"]),
        "w1p": a["L0_ffn_W1p"],
        "w2p": a["L0_ffn_W2p"],
        "wg": a["L1_gnn_weight"],
        "wg_bias": a["L1_gnn_bias"].reshape(1, -1),
        "gate_w": a["L1_ffn_gate_w"],
        "gate_b": np.tile(a["L1_ffn_gate_b"], TB).reshape(1, -1),
        "w1_1": a["L1_ffn_W1"],
        "b1_1": per_partition(a["L1_ffn_b1"]),
        "w2_1": a["L1_ffn_W2"],
        "b2_1": per_partition(a["L1_ffn_b2"]),
    }
    nc = _bacc.Bacc("TRN2", target_bir_lowering=False, num_devices=1, dynamic_dma_scratch_size=4096)
    args, feed = [], {}
    for name, v in arrays.items():
        feed[f"in_{name}"] = np.ascontiguousarray(v)
        args.append(nc.dram_tensor(f"in_{name}", v.shape, _mybir.dt.from_np(v.dtype), kind="ExternalInput").ap())
    args.append(nc.dram_tensor("out_x", [P, NB, D], _mybir.dt.float32, kind="ExternalOutput").ap())
    bass_two_layer_gnn_moe_kernel(nc, *args)
    r = _run(nc, [feed], core_ids=[0])
    got = r.results[0]["out_x"]
    return np.ascontiguousarray(got.transpose(1, 0, 2).reshape(pad, D)[:N])
```

```python
from contextlib import ExitStack

import numpy as np

import concourse.bass as bass
from concourse import mybir

ALU = mybir.AluOpType
ACT = mybir.ActivationFunctionType
F32 = mybir.dt.float32
F32R = mybir.dt.float32r
BF16 = mybir.dt.bfloat16
AX = mybir.AxisListType

N = 5000
P = 128
D = 128
CW = 512
CH = -(-N // CW)
NB = CH * CW // P
TB = CW // P
CLS = 16
E = 8
ALPHA = 0.1
L1_EPS = 1e-12
LN_EPS = 1e-5
LB = 4
LOADS = NB // LB
DEFER = 2
XPER = DEFER * NB // (CH - DEFER)
XB = XPER // DEFER
LAG = 2
M_BUFS = 4
ADJ_BUFS = 5
H_BUFS = 3


A_STEPS = {"aggregate": 0, "residual": 9, "stats": 10, "var": 11, "power": 12, "norm": 13, "turn": 16,
           "copy": 17, "router": 19, "logits": 20, "exp": (21, 22, 23, 24), "top": (26, 27, 28),
           "turn_mask": 30, "copy_mask": 31, "write_mask": 32, "spread": 2, "high": 38, "low": 40}
Z_STEPS = {"last_add": 1, "bias": 1, "edge": 2, "turn_ffn": 4, "close": 4, "store": 10, "load_aux": 3,
           "turn_aux": 7, "copy_aux": 9, "product": 10, "aggregate": 1, "residual": 11, "stats": 12, "var": 13,
           "power": 14, "norm": 16, "turn": 18, "copy": 19, "router": 20, "logits": 21, "exp": (24, 28, 28, 30),
           "top": (31, 31, 34), "turn_mask": 36, "copy_mask": 37, "write_mask": 39, "spread": 2, "high": 37,
           "low": 40}
A_FIRST = {"top": (33, 35, 37), "turn_mask": 39, "copy_mask": 41, "write_mask": 41, "exp": (22, 23, 24, 25)}
Z_FIRST = {}
Z_LAST = {"spread": 1, "top": (29, 31, 35), "residual": 11, "turn": 19, "copy": 20, "router": 21}


class Layer:

    def __init__(self, name, shared, per_expert, down_lag, steps, first, last):
        self.name = name
        self.shared = shared
        self.experts = E + shared
        self.per_expert = per_expert
        self.hidden = self.experts * per_expert
        self.down_lag = down_lag
        self.up_step = [1 + h * (NB - 2) // self.hidden for h in range(self.hidden)]
        self.steps, self.first, self.last = steps, {**steps, **first}, {**steps, **last}
        self.add_step = [self.up_step[(e + 1) * per_expert - 1] + down_lag + 2 for e in range(self.experts - 1 + shared)]

    def at(self, what, k):
        if isinstance(k, int) and k in (1, CH):
            return (self.first if k == 1 else self.last)[what]
        return self.steps[what]

    def down_bank(self, e):
        return e % 2

    def bank_free_count(self, chunk, e):
        same = [x for x in range(e) if self.down_bank(x) == self.down_bank(e)]
        if same:
            return chunk * self.experts + same[-1] + 1
        same = [x for x in range(self.experts) if self.down_bank(x) == self.down_bank(e)]
        return (chunk - 1) * self.experts + same[-1] + 1


def bass_two_layer_gnn_moe_kernel(nc, x_t, adj_in, adj_out, h0_t, y_t, wr0, w1s, b1_0, w2s, b2_0,
                                  w1p, w2p, wg, wg_bias, gate_w, gate_b, w1_1, b1_1, w2_1, b2_1, out):
    ctx = ExitStack()

    place = {}

    def sb(name, shape, dt=F32):
        t = ctx.enter_context(nc.sbuf_tensor(name, shape, dt))
        place[name] = nc.sbuf_base - int(np.prod(shape[1:])) * mybir.dt.size(dt)
        return t

    def over(name, shape, old):
        return nc.alloc_sbuf_tensor_at(name, shape, F32R, offset=place[old])

    def psum(name):
        return ctx.enter_context(nc.psum_tensor(name, [P, CW], F32))

    def sem(name):
        return ctx.enter_context(nc.semaphore(name))

    LA, LZ = Layer("a", 1, 4, 2, A_STEPS, A_FIRST, {}), Layer("b", 0, 2, 4, Z_STEPS, Z_FIRST, Z_LAST)

    xres = sb("xres", [P, NB, D])
    xn = sb("xn", [P, NB, D])
    ysta = sb("ysta", [P, CH * CW], F32R)
    ymov = sb("ymov", [P, 2, CW], F32R)
    w1h = sb("w1h", [P, LA.hidden * P], F32R)
    w1l = sb("w1l", [P, LA.hidden * P], F32R)
    w2 = sb("w2", [P, LA.hidden, D])
    b1 = sb("b1", [P, LA.hidden])
    b2 = sb("b2", [P, LA.experts])
    b1z = sb("b1z", [P, LZ.hidden])
    b2z = sb("b2z", [P, LZ.experts])
    ring = sb("ring", [P, 5, LB * CW])
    late = ring[:, 4, :].rearrange("p (b g n) -> p b g n", b=2, g=2)
    maskb = sb("maskb", [P, E, CW])
    stage = maskb[:].rearrange("p e n -> p (e n)")
    m = sb("m", [P, M_BUFS, CW])
    h = sb("h", [P, H_BUFS, CW])
    wgs = m[:, 0, 0:2 * D].rearrange("p (g o) -> p g o", g=2)
    wedge, wbias, auxf = m[:, 0, 2 * D:3 * D], m[:, 0, 3 * D:4 * D], m[:, 1, :]
    mabs = sb("mabs", [P, 2, CW])
    absum = sb("absum", [P, CW])
    aggf = sb("aggf", [P, CW])
    xnc = sb("xnc", [P, TB, D])
    xnf = sb("xnf", [P, CW])
    xnfh = sb("xnfh", [P, CW], F32R)
    xnfl = sb("xnfl", [P, CW], F32R)
    YP = 2 * CW
    hflat = h[:].rearrange("p b n -> p (b n)")
    ffn = sb("ffn", [P, CW])
    term = sb("term", [P, CW])
    aux = sb("aux", [P, TB, D])
    xnext = sb("xnext", [P, TB, D])
    junk = sb("junk", [P, 2, CW], BF16)
    ident = sb("ident", [P, P])
    ones = sb("ones", [P, 1])
    wr = sb("wr", [P, 2, E])
    gateb = sb("gateb", [P, TB, E])
    stats = sb("stats", [P, 2 * TB, 6])
    stats0 = term[:, 0:NB * 6].rearrange("p (b s) -> p b s", b=NB)
    mv = sb("mv", [P, NB, 2])
    vareps = sb("vareps", [P, NB])
    rstd = sb("rstd", [P, NB])
    mhalf = sb("mhalf", [P, NB])
    redge = sb("redge", [P, NB])
    rpart = sb("rpart", [P, NB])
    xpart = sb("xpart", [P, XPER])
    rl = sb("rl", [P, TB])
    rinv = sb("rinv", [P, TB])
    lg = sb("lg", [P, TB, E])
    ex = sb("ex", [P, TB, E])
    ex2 = sb("ex2", [P, TB, E])
    rank = sb("rank", [P, TB, E])
    first = sb("first", [P, TB, E])
    second = sb("second", [P, TB, E])
    prio = sb("prio", [P, TB, E])
    mask = sb("mask", [P, TB, E])
    euler = sb("euler", [P, TB, E])
    red = sb("red", [P, TB])
    red2 = sb("red2", [P, TB])
    maskt = sb("maskt", [E, CW])

    WZ = LZ.hidden * P
    xnh = ysta[:].rearrange("p (b d) -> p b d", b=NB)
    def xnl_chunk(c):
        t, at = ((w1h, WZ + c * CW) if c < CH // 2 else (w1l, WZ + (c - CH // 2) * CW))
        return t[:, at:at + CW]

    def xnl(b):
        return xnl_chunk(b // TB)[:, b % TB * D:(b % TB + 1) * D]
    adj_over_w2 = over("adj_over_w2", [P, 2, 4, CW], "w2")
    adj_over_m = nc.alloc_sbuf_tensor_at("adj_over_m", [P, 2, CW], F32R, offset=place["m"] + 2 * CW * 4)

    def adj_part(low, b):
        return adj_over_w2[:, low, b % ADJ_BUFS, :] if b % ADJ_BUFS < 4 else adj_over_m[:, low, :]

    w2_parts = over("w2_parts", [P, 2, WZ], "xn")
    w2h, w2l = w2_parts[:, 0, :], w2_parts[:, 1, :]
    hh = nc.alloc_sbuf_tensor_at("hh", [P, 2, CW], F32R, offset=place["xn"] + 2 * WZ * 4)
    hl = over("hl", [P, 2, CW], "mabs")

    sbank = [psum("s0"), psum("s1")]
    abank = psum("agg")
    ubank = [psum("u0"), psum("u1")]
    dbank = [psum("d0"), psum("d1")]
    misc = psum("misc")

    mask_dram = nc.dram_tensor("mask_scratch", [2, CH, E, CW], F32, kind="Internal").ap()
    xn_dram = nc.dram_tensor("xn_scratch", [P, NB, D], F32, kind="Internal").ap()

    consts_set = sem("consts_set")
    ident_zeroed = sem("ident_zeroed")
    x_landed = [sem(f"x_landed{i}") for i in range(4)]
    weights_landed = sem("weights_landed")
    up_landed = sem("up_landed")
    up_high = sem("up_high")
    up_split = sem("up_split")
    small_landed = sem("small_landed")
    yraw_landed = [sem(f"yraw_landed{i}") for i in range(3)]
    y_high = sem("y_high")
    y_split = sem("y_split")
    ymov_landed = sem("ymov_landed")
    dve_carried, pool_carried, sp_carried = sem("dve_carried"), sem("pool_carried"), sem("sp_carried")
    setup_chain = sem("setup_chain")
    setup_rstd = sem("setup_rstd")
    xn_ready = sem("xn_ready")
    xn_written = sem("xn_written")
    xn_landed = sem("xn_landed")
    xn_last_landed = sem("xn_last_landed")
    xn_high = sem("xn_high")
    xn_low, xn_low_odd = sem("xn_low"), sem("xn_low_odd")
    adj_high, adj_low = sem("adj_high"), sem("adj_low")
    h_high, h_low = sem("h_high"), sem("h_low")
    w2_high, w2_split = sem("w2_high"), sem("w2_split")
    aux_landed = sem("aux_landed")
    weights2_landed = sem("weights2_landed")
    graph_weights_landed = sem("graph_weights_landed")
    ring_landed = [sem(f"ring_landed{i}") for i in range(4)]
    ring2_landed = [sem(f"ring2_landed{i}") for i in range(5)]
    late_landed = [sem(f"late_landed{i}") for i in range(2)]
    late_read = sem("late_read")
    out_written = sem("out_written")
    h0_landed = sem("h0_landed")
    redge_chain = sem("redge_chain")
    edges_read = sem("edges_read")
    s_made = sem("s_made")
    m_made = sem("m_made")
    abs_made = sem("abs_made")
    abs_added = sem("abs_added")
    rowsum_made = sem("rowsum_made")
    rl_chain = sem("rl_chain")
    auxf_made = sem("auxf_made")
    aux_turned = sem("aux_turned")

    NAMES = ["agg_blocks",
             "aggf_made", "agg_turned", "up_made", "gelu_made", "down_made", "experts_added", "term_made",
             "mid_chain", "mid_var", "mid_rstd", "xnc_made", "xnc_turned", "xnf_made", "xnf_high", "xnf_split", "router_made",
             "lg_made", "router_chain", "exp_made", "mask_chain", "mask_made", "mask_turned", "maskt_made",
             "mask_written", "maskb_landed", "ffn_turned", "end_chain", "end_var", "end_rstd",
             "xnext_made", "xnext_written"]
    SA = {n: sem("a_" + n) for n in NAMES}
    SZ = {n: sem("b_" + n) for n in NAMES}

    def wait(eng, s, value):
        if isinstance(value, int) and value <= 0:
            return
        eng.wait_ge(s, value)

    def carry(eng, s):
        eng.sem_inc(s, 1)

    def cols(chunk):
        return bass.ds(chunk * CW, CW)

    def blks(chunk):
        return bass.ds(chunk * TB, TB)

    def pipeline(eng, iteration, to=CH + 3):
        for k in range(3):
            iteration(k, True, k >= 1, k >= 2, False)
        with eng.Fori(3, CH) as k:
            iteration(k, True, True, True, True)
        iteration(CH, False, True, True, True)
        iteration(CH + 1, False, False, True, True)
        if to == CH + 3:
            iteration(CH + 2, False, False, False, True)

    def split_low(eng, low, raw, high):
        return eng.tensor_tensor(low, raw, high.bitcast(F32), ALU.subtract)

    def lows_on_vector(k):
        return isinstance(k, int) and k >= CH

    def hidden_low(eng, k, s):
        for hb in range(LZ.hidden):
            if LZ.up_step[hb] == s - 2:
                n = (k - 2) * LZ.hidden + hb
                wait(eng, h_high, n + 1)
                if lows_on_vector(k):
                    wait(eng, h_low, n)
                split_low(eng, hl[:, hb % 2, :], h[:, hb % H_BUFS, :], hh[:, hb % 2, :]).then_inc(h_low, 1)

    def adds_on_vector(k, b):
        return isinstance(k, int) and (k == 0 and b % 4 == 0 or k == 1 and b % 2 == 0)

    def add_abs(eng, k, b):
        wait(eng, abs_made, k * NB + b + 1)
        wait(eng, abs_added, k * (NB - 1) + b - 1)
        eng.tensor_tensor(absum[:], mabs[:, b % 2, :], absum[:], ALU.add).then_inc(abs_added, 1)

    def norm_chunk_low(eng, c, done):
        eng.wait_ge(xn_high, c + 1)
        eng.wait_ge(xn_last_landed if c == CH - 1 else xn_landed, 16)
        split_low(eng, xnl_chunk(c), xn[:, c * TB:(c + 1) * TB, :].rearrange("p b d -> p (b d)"),
                  ysta[:, c * CW:(c + 1) * CW]).then_inc(done, 1)

    STEPS = NB + LAG + 1
    Y_PIECES = CH * CW // YP
    Y_BLOCKS = YP // P

    def only_in(k):
        return isinstance(k, int) and k < DEFER

    def in_slot(k, l):
        return (k * LOADS + l) % 4 if only_in(k) else l % 2

    def in_count(k, l):
        if only_in(k):
            return 16 * ((k * LOADS + l) // 4 + 1)
        return 16 * (DEFER * LOADS // 4 + (k - DEFER) * (LOADS // 2) + l // 2 + 1)

    def up_weights(e):
        raw = ffn[:] if e < LA.shared else maskb[:, e - LA.shared, :]
        return raw, slice(e * LA.per_expert * P, (e + 1) * LA.per_expert * P)

    def y_piece(c):
        raw = hflat[:, 0:YP] if c == 0 else stage[:, (c - 1) * YP:c * YP]
        return raw, slice(c * YP, (c + 1) * YP)

    block = ctx.enter_context(nc.Block())

    @block.sync
    def _(sp):
        def load_x(i):
            sp.dma_start(xres[:, i * 10:(i + 1) * 10, :], x_t[:, i * 10:(i + 1) * 10, :]).then_inc(x_landed[i], 16)

        def load_in(k, l):
            sp.dma_start(ring[:, in_slot(k, l), :], adj_in[k, :, l * LB * CW:(l + 1) * LB * CW]
                         ).then_inc(ring_landed[in_slot(k, l)], 16)

        def both_loads(k, l):
            wait(sp, edges_read, (k - DEFER) * NB + (l - 1) * LB)
            load_in(k, l)
            if isinstance(k, int) and l < 2:
                sp.wait_ge(m_made, (k * LOADS + l - 1) * LB)
            sp.dma_start(ring[:, 2 + l % 2, :], adj_out[k, :, l * LB * CW:(l + 1) * LB * CW]
                         ).then_inc(ring_landed[2 + l % 2], 16)

        def late_loads(k, i):
            b = (k - DEFER) * XB + i % XB
            wait(sp, late_read, (k - DEFER) * XPER + i - 1)
            carry(sp, sp_carried)
            for g, adj in enumerate((adj_in, adj_out)):
                sp.dma_start(late[:, i % 2, g, :], adj[i // XB, :, bass.ds(b * CW, CW)]
                             ).then_inc(late_landed[i % 2], 16)

        def load_ymov(k, buf):
            wait(sp, s_made, (k - 1) * NB)
            carry(sp, sp_carried)
            wait(sp, ymov_landed, 64 * k)
            carry(sp, sp_carried)
            for dst, src in enumerate((0, 2, 1, 3)):
                sp.dma_start(ymov[32 * dst:32 * dst + 32, buf, :].bitcast(F32),
                             ysta[32 * src:32 * src + 32, cols(k)].bitcast(F32)
                             ).then_inc(ymov_landed, 16)

        def load_y(first, last, landed):
            n = (last - first) * YP
            dst = hflat[:, 0:YP] if first == 0 else stage[:, (first - 1) * YP:(last - 1) * YP]
            for g in range(4):
                sp.dma_start(dst[32 * g:32 * g + 32, :], y_t[:, first * YP:first * YP + n]).then_inc(landed, 16)

        load_y(0, 1, yraw_landed[0])
        load_x(0)
        load_in(0, 0)
        load_y(1, 2, yraw_landed[1])
        sp.wait_ge(y_split, 1)
        load_ymov(0, 0)
        load_x(1)
        load_in(0, 1)
        load_in(0, 2)
        load_y(2, Y_PIECES, yraw_landed[2])
        load_x(2)
        load_in(0, 3)
        load_x(3)
        for i, (dst, src) in enumerate(((b1, b1_0), (b2, b2_0), (b1z, b1_1), (b2z, b2_1))):
            sp.dma_start(dst[:], src).then_inc(small_landed, 16)
        sp.dma_start(wr[:, 0, :], wr0).then_inc(small_landed, 16)
        sp.dma_start(wr[:, 1, :], gate_w).then_inc(small_landed, 16)
        sp.dma_start(gateb[:], gate_b.to_broadcast([P, TB * E]).rearrange("p (t e) -> p t e", t=TB)
                     ).then_inc(small_landed, 16)
        for k in range(DEFER):
            if k == 1:
                load_ymov(1, 1)
            for l in range(0 if k else 4, LOADS):
                wait(sp, m_made, (k * LOADS + l - 3) * LB)
                load_in(k, l)
                if k == 1 and l == 2:
                    sp.wait_ge(y_split, Y_PIECES)
                    sp.dma_start(ffn[:], w1s).then_inc(up_landed, 16)
                    sp.dma_start(maskb[:], w1p.rearrange("e d f -> d e f")).then_inc(up_landed, 16)
            if k == 1:
                sp.dma_start(w2[:, 0:LA.per_expert, :], w2s.rearrange("(k p) d -> p k d", p=P)
                             ).then_inc(weights_landed, 16)
                sp.dma_start(w2[:, LA.per_expert:, :], w2p.rearrange("e (k p) d -> p (e k) d", p=P)
                             ).then_inc(weights_landed, 16)

        def loads_of(k, buf):
            load_ymov(k, buf)
            for l in range(LOADS):
                if isinstance(k, int) and l < 2:
                    sp.wait_ge(m_made, (k * LOADS + l - 3) * LB)
                both_loads(k, l)
                for i in range(l * XPER // LOADS, (l + 1) * XPER // LOADS):
                    late_loads(k, i)

        loads_of(DEFER, DEFER % 2)
        with sp.Fori(DEFER + 1, CH) as k:
            loads_of(k, sp.snap(k % 2))

        sp.wait_ge(edges_read, (CH - DEFER) * NB)
        sp.wait_ge(late_read, DEFER * NB)
        for l in range(5):
            sp.dma_start(ring[:, l, :], adj_in[0, :, l * LB * CW:(l + 1) * LB * CW]).then_inc(ring2_landed[l], 16)
        sp.wait_ge(SA["agg_blocks"], CH * NB)
        sp.wait_ge(SA["xnext_written"], 16 * (CH - 1))
        sp.dma_start(xn[:, 0:NB - TB, :], xn_dram[:, 0:NB - TB, :]).then_inc(xn_landed, 16)
        sp.wait_ge(abs_made, CH * NB)
        sp.dma_start(wgs, wg[0:2 * D, :].rearrange("(g d) o -> d g o", g=2)).then_inc(graph_weights_landed, 16)
        sp.dma_start(wedge, wg[2 * D:2 * D + 1, :].to_broadcast([P, D])).then_inc(graph_weights_landed, 16)
        sp.dma_start(wbias, wg_bias.to_broadcast([P, D])).then_inc(graph_weights_landed, 16)

        def z_load(k, l):
            wait(sp, adj_low, k * NB + (l - 4) * LB)
            sp.dma_start(ring[:, l % 5, :], adj_in[k, :, l * LB * CW:(l + 1) * LB * CW]
                         ).then_inc(ring2_landed[l % 5], 16)

        for l in range(5, LOADS):
            z_load(0, l)
        with sp.Fori(1, CH) as k:
            for l in range(LOADS):
                z_load(k, l)

    @block.tensor
    def _(pe):
        def transposes(src, done):
            for t in range(TB):
                last = pe.transpose(misc[:, t * P:(t + 1) * P], src(t), ident[:])
            last.then_inc(done, 1)

        def up(L, S, j, hb):
            if hb == 0:
                wait(pe, S["xnf_split"], j + 1)
            wait(pe, S["gelu_made"], j * L.hidden + hb - 1)
            at, u = slice(hb * P, (hb + 1) * P), ubank[hb % 2]
            pe.matmul(u[:], w1h[:, at], xnfh[:], start=True, stop=False)
            pe.matmul(u[:], w1h[:, at], xnfl[:], start=False, stop=False)
            pe.matmul(u[:], w1l[:, at], xnfh[:], start=False, stop=True).then_inc(S["up_made"], 1)

        def down(L, S, j, hb):
            e, part = divmod(hb, L.per_expert)
            d, at, first, last = dbank[L.down_bank(e)], slice(hb * D, (hb + 1) * D), part == 0, part == L.per_expert - 1
            if first:
                wait(pe, S["experts_added"], L.bank_free_count(j, e))
            if L is LZ:
                wait(pe, h_low, j * L.hidden + hb + 1)
                pe.matmul(d[:], w2h[:, at], hh[:, hb % 2, :], start=first, stop=False)
                pe.matmul(d[:], w2h[:, at], hl[:, hb % 2, :], start=False, stop=False)
                pe.matmul(d[:], w2l[:, at], hh[:, hb % 2, :], start=False, stop=last).then_inc(S["down_made"], 1)
                return
            wait(pe, S["gelu_made"], j * L.hidden + hb + 1)
            pe.matmul(d[:], w2[:, hb, :], h[:, hb % H_BUFS, :], start=first, stop=last).then_inc(S["down_made"], 1)

        def hidden_at(L, s):
            return [hb for hb in range(L.hidden) if L.up_step[hb] == s]

        def turn_ffn(L, S, j):
            wait(pe, S["experts_added"], (j + 1) * L.experts)
            transposes(lambda t: ffn[:, t * P:(t + 1) * P], S["ffn_turned"])

        def turn_mask(L, S, j):
            wait(pe, S["mask_made"], j + 1)
            for t in range(TB):
                last = pe.transpose(misc[0:E, t * P:(t + 1) * P], mask[:, t, :], ident[:])
            last.then_inc(S["mask_turned"], 1)

        def turn_norm(L, S, j):
            wait(pe, S["xnc_made"], j + 1)
            transposes(lambda t: xnc[:, t, :], S["xnc_turned"])

        def router(L, S, j, which):
            wait(pe, S["xnf_made"], j + 1)
            for t in range(TB):
                last = pe.matmul(misc[:, t * E:(t + 1) * E], xnf[:, t * P:(t + 1) * P], wr[:, which, :],
                                 start=True, stop=True)
            last.then_inc(S["router_made"], 1)

        def a_end(k, s, mid, run_ffn):
            if s == 4:
                if mid:
                    wait(pe, rl_chain, 3 * (k - 1) + 1)
                else:
                    wait(pe, SA["maskt_made"], k - 1 if run_ffn else k - 2)
                turn_ffn(LA, SA, k - 3)

        def a_iteration(k, agg, mid, run_ffn, end):
            L, S = LA, SA
            for s in range(STEPS):
                if agg and s < NB:
                    if s == 0:
                        wait(pe, ymov_landed, 64 * (k + 1))
                    if isinstance(k, int) and k == 0 and s % Y_BLOCKS == 0:
                        pe.wait_ge(y_split, s // Y_BLOCKS + 1)
                    wait(pe, m_made, k * NB + s - 1)
                    pe.matmul(sbank[s % 2][:], ysta[:, s * P:(s + 1) * P], ymov[:, k % 2, :],
                              start=True, stop=True).then_inc(s_made, 1)
                if run_ffn:
                    if isinstance(k, int) and k == 2 and s == 0:
                        pe.wait_ge(up_split, LA.experts)
                        pe.wait_ge(weights_landed, 32)
                    for hb in hidden_at(L, s):
                        up(L, S, k - 2, hb)
                if agg and LAG <= s < NB + LAG:
                    b = s - LAG
                    if b == 0:
                        wait(pe, S["aggf_made"], k)
                    if isinstance(k, int) and k == 0 and b % 2 == 0:
                        pe.wait_ge(xn_ready, b // 2 + 1)
                    wait(pe, m_made, k * NB + b + 1)
                    pe.matmul(abank[:], xn[:, b, :], m[:, b % M_BUFS, :], start=b == 0, stop=b == NB - 1
                              ).then_inc(S["agg_blocks"], 1)
                if run_ffn:
                    for hb in hidden_at(L, s - L.down_lag):
                        down(L, S, k - 2, hb)
                if isinstance(k, int) and k == 1 and s == 0:
                    pe.wait_ge(consts_set, 1)
                    pe.wait_ge(small_landed, 16 * 7)
                if mid and s == 1:
                    j = k - 1
                    wait(pe, abs_added, k * (NB - 1))
                    wait(pe, S["maskt_made"], j)
                    for t in range(TB):
                        last = pe.matmul(misc[:, t:t + 1], absum[:, t * P:(t + 1) * P], ones[:],
                                         start=True, stop=True)
                    last.then_inc(rowsum_made, 1)
                if end:
                    a_end(k, s, mid, run_ffn)
                if mid and s == 7:
                    j = k - 1
                    if end:
                        wait(pe, S["end_chain"], 3 * (k - 3) + 1)
                    wait(pe, rl_chain, 3 * j + 1)
                    wait(pe, S["aggf_made"], j + 1)
                    transposes(lambda t: aggf[:, t * P:(t + 1) * P], S["agg_turned"])
                if mid and s == L.at("turn", k):
                    turn_norm(L, S, k - 1)
                if mid and s == L.at("router", k):
                    router(L, S, k - 1, 0)
                if mid and s == L.at("turn_mask", k):
                    turn_mask(L, S, k - 1)

        pipeline(pe, a_iteration, CH + 2)

        def z_iteration(k, agg, mid, run_ffn, end):
            L, S = LZ, SZ
            for s in range(STEPS):
                if run_ffn:
                    if isinstance(k, int) and k == 2 and s == 0:
                        pe.wait_ge(up_split, LA.experts + 1)
                        pe.wait_ge(w2_split, 1)
                    for hb in hidden_at(L, s):
                        up(L, S, k - 2, hb)
                if agg and LAG <= s < NB + LAG:
                    b = s - LAG
                    if b == 0:
                        wait(pe, S["aggf_made"], k)
                    if isinstance(k, int) and k == 0 and b % TB == 0:
                        c = b // TB
                        pe.wait_ge(xn_low_odd if c % 2 else xn_low, c // 2 + 1)
                    wait(pe, adj_low, k * NB + b + 1)
                    hi, lo = adj_part(0, b), adj_part(1, b)
                    pe.matmul(abank[:], xnh[:, b, :], hi, start=b == 0, stop=False)
                    pe.matmul(abank[:], xnh[:, b, :], lo, start=False, stop=False)
                    pe.matmul(abank[:], xnl(b), hi, start=False, stop=b == NB - 1).then_inc(S["agg_blocks"], 1)
                if run_ffn:
                    for hb in hidden_at(L, s - L.down_lag):
                        down(L, S, k - 2, hb)
                if isinstance(k, int) and k == 0:
                    a_end(CH + 2, s, False, False)
                if isinstance(k, int) and k == 1 and s == 0:
                    pe.wait_ge(SA["xnext_made"], CH)
                if end and s == L.at("turn_ffn", k):
                    wait(pe, S["maskt_made"], k - 1 if run_ffn else k - 2)
                    turn_ffn(L, S, k - 3)
                if mid and s == L.at("turn_aux", k):
                    j = k - 1
                    wait(pe, S["maskt_made"], k - 1)
                    if end:
                        wait(pe, S["xnext_made"], k - 2)
                    wait(pe, aux_landed, 16 * (j + 1))
                    transposes(lambda t: aux[:, t, :], aux_turned)
                if mid and s == L.at("product", k):
                    j = k - 1
                    wait(pe, auxf_made, j + 1)
                    wait(pe, S["aggf_made"], j + 1)
                    if isinstance(k, int) and k == 1:
                        pe.wait_ge(graph_weights_landed, 48)
                    for t in range(TB):
                        pe.matmul(misc[:, t * P:(t + 1) * P], auxf[:, t * P:(t + 1) * P], wgs[:, 0, :],
                                  start=True, stop=False)
                        last = pe.matmul(misc[:, t * P:(t + 1) * P], aggf[:, t * P:(t + 1) * P], wgs[:, 1, :],
                                         start=False, stop=True)
                    last.then_inc(S["agg_turned"], 1)
                if mid and s == L.at("turn", k):
                    turn_norm(L, S, k - 1)
                if mid and s == L.at("router", k):
                    router(L, S, k - 1, 1)
                if mid and s == L.at("turn_mask", k):
                    turn_mask(L, S, k - 1)

        pipeline(pe, z_iteration)

    @block.scalar
    def _(act):
        def gelu(L, S, j, hb, bias):
            wait(act, S["up_made"], j * L.hidden + hb + 1)
            wait(act, h_low if L is LZ else S["down_made"], j * L.hidden + hb + 1 - H_BUFS)
            act.activation(h[:, hb % H_BUFS, :], ubank[hb % 2][:], ACT.Gelu, bias=bias[:, hb:hb + 1]
                           ).then_inc(S["gelu_made"], 1)

        def y_high_copy(c):
            act.wait_ge(yraw_landed[min(c, 2)], 16 * 4)
            raw, at = y_piece(c)
            act.copy(ysta[:, at], raw).then_inc(y_high, 1)

        def iteration(L, S, k, agg, mid, run_ffn, bias):
            j = k - 1
            for s in range(STEPS):
                if L is LA and isinstance(k, int) and k == 0 and s % Y_BLOCKS == 0 and s // Y_BLOCKS + 1 < Y_PIECES:
                    y_high_copy(s // Y_BLOCKS + 1)
                if L is LA and isinstance(k, int) and k == 1 and 20 <= s < 20 + LA.experts:
                    act.wait_ge(up_landed, 32)
                    raw, at = up_weights(s - 20)
                    act.copy(w1h[:, at], raw).then_inc(up_high, 1)
                    if s == 20:
                        act.wait_ge(small_landed, 16 * 7)
                if L is LZ and agg and s < NB:
                    if isinstance(k, int) and k == 0 and s % TB == 0:
                        c = s // TB
                        act.wait_ge(xn_last_landed if c == CH - 1 else xn_landed, 16)
                        act.copy(xnh[:, c * TB:(c + 1) * TB, :], xn[:, c * TB:(c + 1) * TB, :]).then_inc(xn_high, 1)
                    l = s // LB
                    if s % LB == 0:
                        wait(act, ring2_landed[l % 5], 16 * (k * (LOADS // 5) + l // 5 + 1))
                    wait(act, S["agg_blocks"], k * NB + s + 1 - ADJ_BUFS)
                    act.copy(adj_part(0, s), ring[:, l % 5, (s % LB) * CW:(s % LB + 1) * CW]
                             ).then_inc(adj_high, 1)
                if L is LZ and isinstance(k, int) and k == 0 and s == 5:
                    act.wait_ge(SA["experts_added"], CH * LA.experts)
                    act.dma_start(stage[:, 0:WZ].rearrange("p (e f) -> p e f", e=E), w1_1.rearrange("e d f -> d e f")
                                  ).then_inc(up_landed, 16)
                    act.dma_start(stage[:, WZ:2 * WZ].rearrange("p (k d) -> p k d", d=D),
                                  w2_1.rearrange("e (k p) d -> p (e k) d", p=P)).then_inc(weights2_landed, 16)
                if L is LZ and isinstance(k, int) and k == 1 and s == 3:
                    act.wait_ge(up_landed, 48)
                    act.copy(w1h[:, 0:WZ], stage[:, 0:WZ]).then_inc(up_high, 1)
                if L is LZ and isinstance(k, int) and k == 1 and s == 14:
                    act.wait_ge(weights2_landed, 16)
                    act.wait_ge(xn_low, CH // 2)
                    act.wait_ge(xn_low_odd, CH // 2)
                    act.copy(w2h, stage[:, WZ:2 * WZ]).then_inc(w2_high, 1)
                if mid and s == L.at("aggregate", k):
                    wait(act, S["agg_blocks"], k * NB)
                    wait(act, S["agg_turned"], j)
                    act.copy(aggf[:], abank[:]).then_inc(S["aggf_made"], 1)
                if run_ffn:
                    for hb in range(L.hidden):
                        if L is LZ and L.up_step[hb] == s - 1:
                            n = (k - 2) * L.hidden + hb
                            wait(act, S["gelu_made"], n + 1)
                            wait(act, S["down_made"], n - 1)
                            act.copy(hh[:, hb % 2, :], h[:, hb % H_BUFS, :]).then_inc(h_high, 1)
                        if L.up_step[hb] == s:
                            gelu(L, S, k - 2, hb, bias)
                if S is SA and agg and 1 <= s <= NB:
                    b = s - 1
                    wait(act, m_made, k * NB + b + 1)
                    if b == 0:
                        wait(act, rowsum_made, k)
                    else:
                        wait(act, abs_added, k * (NB - 1) + max(b - 2, 0))
                    act.activation(mabs[:, b % 2, :] if b else absum[:], m[:, b % M_BUFS, :], ACT.Abs
                                   ).then_inc(abs_made, 1)
                if run_ffn and s == L.at("spread", k):
                    spread_mask(L, S, k - 2)
                if mid and s == L.at("copy_mask", k):
                    wait(act, S["mask_turned"], j + 1)
                    wait(act, S["mask_written"], 16 * j)
                    act.copy(maskt[:], misc[0:E, :]).then_inc(S["maskt_made"], 1)
                if mid and s == L.at("write_mask", k):
                    wait(act, S["maskt_made"], j + 1)
                    act.dma_start(mask_dram[0 if L is LA else 1, bass.ds(j, 1)].rearrange("o e n -> (o e) n"), maskt[:]
                                  ).then_inc(S["mask_written"], 16)
                if mid and L is LZ and s == L.at("copy_aux", k):
                    wait(act, aux_turned, j + 1)
                    wait(act, S["agg_turned"], j)
                    wait(act, abs_made, CH * NB)
                    act.copy(auxf, misc[:]).then_inc(auxf_made, 1)
                if mid and s == L.at("copy", k):
                    wait(act, S["xnc_turned"], j + 1)
                    wait(act, S["xnf_split"], j)
                    act.copy(xnf[:], misc[:]).then_inc(S["xnf_made"], 1)
                if mid and s == L.at("high", k):
                    wait(act, S["xnf_made"], j + 1)
                    if run_ffn:
                        wait(act, S["up_made"], (k - 1) * L.hidden)
                    act.copy(xnfh[:], xnf[:]).then_inc(S["xnf_high"], 1)

        def spread_mask(L, S, j):
            wait(act, S["mask_written"], 16 * (j + 1))
            wait(act, S["experts_added"], L.experts * j)
            if L is LA:
                act.wait_ge(up_split, LA.experts)
            else:
                act.wait_ge(up_split, LA.experts + 1)
                act.wait_ge(w2_split, 1)
            act.dma_start(maskb[:].rearrange("p e n -> p (e n)"),
                          mask_dram[0 if L is LA else 1, bass.ds(j, 1)].rearrange("o e n -> o (e n)")
                          .to_broadcast([P, E * CW])).then_inc(S["maskb_landed"], 16)

        y_high_copy(0)
        pipeline(act, lambda k, agg, mid, run_ffn, end: iteration(LA, SA, k, agg, mid, run_ffn, b1), CH + 2)
        act.wait_ge(SA["down_made"], CH * LA.hidden)
        act.wait_ge(s_made, CH * NB)
        pipeline(act, lambda k, agg, mid, run_ffn, end: iteration(LZ, SZ, k, agg, mid, run_ffn, b1z))

    @block.vector
    def _(dve):
        def norm_stats(stat_at, src, chain):
            carry(dve, dve_carried)
            for t in range(TB):
                last = dve.bn_stats(stats[:, stat_at + t, :], src(t))
            last.then_inc(chain, 1)

        def norm_var(stat_at, chain, base, var_ready):
            dve.wait_ge(chain, base + 1)
            carry(dve, dve_carried)
            for t in range(TB):
                last = dve.bn_aggr(mv[:, stat_at + t, :], stats[:, stat_at + t, :])
            last.then_inc(chain, 1)
            dve.wait_ge(chain, base + 2)
            dve.tensor_scalar(vareps[:, stat_at:stat_at + TB], mv[:, stat_at:stat_at + TB, 1], LN_EPS, None, ALU.add
                              ).then_inc(var_ready, 1)

        def norm_apply(stat_at, src, dst, rstd_ready, count, done):
            dve.wait_ge(rstd_ready, count)
            for t in range(TB):
                last = dve.tensor_scalar(dst[:, t, :], src(t), mv[:, stat_at + t, 0:1],
                                         rstd[:, stat_at + t:stat_at + t + 1], ALU.subtract, ALU.mult)
            last.then_inc(done, 1)

        def rows_of(j):
            return lambda t: xres[:, bass.ds(j * TB + t, 1), :].rearrange("p o d -> p (o d)")

        def norm_low(S, j):
            wait(dve, S["xnf_high"], j + 1)
            wait(dve, S["xnf_made"], j + 1)
            split_low(dve, xnfl[:], xnf[:], xnfh[:]).then_inc(S["xnf_split"], 1)

        def router_logits(S, j, biased):
            wait(dve, S["router_made"], j + 1)
            wait(dve, S["exp_made"], TB * j)
            v = misc[:, 0:TB * E].rearrange("p (t e) -> p t e", t=TB)
            if biased:
                dve.tensor_tensor(lg[:], v, gateb[:], ALU.add).then_inc(S["router_chain"], 1)
            else:
                dve.tensor_copy(lg[:], v).then_inc(S["router_chain"], 1)
            wait(dve, S["router_chain"], 2 * j + 1)
            dve.tensor_reduce(red2[:], lg[:], AX.X, ALU.max).then_inc(S["router_chain"], 1)
            wait(dve, S["router_chain"], 2 * j + 2)
            dve.tensor_tensor(lg[:], lg[:], spread(red2), ALU.subtract).then_inc(S["lg_made"], 1)

        def spread(r):
            return r[:].unsqueeze(2).to_broadcast([P, TB, E])

        TOP_STEPS = 15

        def top_two(S, j, part, over_all):
            count = [(0, 6, 11)[part]]

            def step(ins):
                count[0] += 1
                ins.then_inc(S["mask_chain"], 1)
                dve.wait_ge(S["mask_chain"], TOP_STEPS * j + count[0])

            def one_hot(dst, src):
                step(dve.tensor_reduce(red[:], src[:], AX.X, ALU.max))
                step(dve.tensor_tensor(rank[:], src[:], spread(red), ALU.is_equal))
                step(dve.tensor_tensor(rank[:], rank[:], prio[:], ALU.mult))
                step(dve.tensor_reduce(red[:], rank[:], AX.X, ALU.max))
                step(dve.tensor_tensor(dst[:], rank[:], spread(red), ALU.is_equal))

            if part == 0:
                wait(dve, S["exp_made"], TB * (j + 1))
                wait(dve, S["mask_turned"], j)
                one_hot(first, ex)
                step(dve.scalar_tensor_tensor(ex2[:], first[:], -2.0, ex[:], ALU.mult, ALU.add))
            elif part == 1:
                one_hot(second, ex2)
            else:
                step(dve.tensor_tensor(second[:], first[:], second[:], ALU.add))
                step(dve.tensor_tensor(second[:], second[:], ex[:], ALU.mult))
                step(dve.tensor_reduce(red[:], (ex if over_all else second)[:], AX.X, ALU.add))
                step(dve.reciprocal(red2[:], red[:]))
                assert count[0] == TOP_STEPS
                dve.tensor_tensor(mask[:], second[:], spread(red2), ALU.mult).then_inc(S["mask_made"], 1)

        def router_parts(L, S, s, k, j, biased):
            if s == L.at("logits", k):
                router_logits(S, j, biased)
            for part in range(3):
                if s == L.at("top", k)[part]:
                    top_two(S, j, part, biased)
            if s == L.at("low", k):
                norm_low(S, j)

        def add_expert(L, S, j, e, bias):
            wait(dve, S["down_made"], j * L.hidden + (e + 1) * L.per_expert)
            d = dbank[L.down_bank(e)]
            if e == 0:
                wait(dve, S["ffn_turned"], j)
            if e < L.shared:
                dve.tensor_scalar(ffn[:], d[:], bias[:, e:e + 1], None, ALU.add).then_inc(S["experts_added"], 1)
                return
            r = e - L.shared
            if r == 0:
                wait(dve, S["maskb_landed"], 16 * (j + 1))
            if e == 0:
                dve.scalar_tensor_tensor(ffn[:], d[:], bias[:, e:e + 1], maskb[:, r, :], ALU.add, ALU.mult
                                         ).then_inc(S["experts_added"], 1)
                return
            wait(dve, S["experts_added"], j * L.experts + e)
            dve.scalar_tensor_tensor(term[:], d[:], bias[:, e:e + 1], maskb[:, r, :], ALU.add, ALU.mult
                                     ).then_inc(S["term_made"], 1)
            wait(dve, S["term_made"], j * (L.experts - 1) + e)
            dve.tensor_tensor(ffn[:], ffn[:], term[:], ALU.add).then_inc(S["experts_added"], 1)

        def input_stats(i, part):
            if part == 0:
                dve.wait_ge(x_landed[i], 16)
            for b in (i * 10 + 2 * part, i * 10 + 2 * part + 1):
                last = dve.bn_stats(stats0[:, b, :], xres[:, b, :])
            if part == 4:
                last.then_inc(setup_chain, 1)

        def input_var(i):
            piece = slice(i * 10, i * 10 + 10)
            dve.wait_ge(setup_chain, 3 * i + 1)
            for b in range(i * 10, i * 10 + 10):
                last = dve.bn_aggr(mv[:, b, :], stats0[:, b, :])
            last.then_inc(setup_chain, 1)
            dve.wait_ge(setup_chain, 3 * i + 2)
            dve.tensor_scalar(vareps[:, piece], mv[:, piece, 1], LN_EPS, None, ALU.add).then_inc(setup_chain, 1)

        def input_norm(i, part):
            dve.wait_ge(setup_rstd, i + 1)
            for b in (i * 10 + 2 * part, i * 10 + 2 * part + 1):
                last = dve.tensor_scalar(xn[:, b, :], xres[:, b, :], mv[:, b, 0:1], rstd[:, b:b + 1],
                                         ALU.subtract, ALU.mult)
            last.then_inc(xn_ready, 1)

        def y_low(c):
            dve.wait_ge(y_high, c + 1)
            raw, at = y_piece(c)
            split_low(dve, ysta[64:128, at], raw[64:128, :], ysta[64:128, at]).then_inc(y_split, 1)

        dve.memset(redge[:], 0.0).then_inc(redge_chain, 1)
        y_low(0)
        for part in range(5):
            input_stats(0, part)
        input_var(0)

        def a_end(k, s):
            S, j = SA, k - 3
            if s == 5:
                wait(dve, S["ffn_turned"], j + 1)
                dve.tensor_tensor(xres[:, blks(j), :], xres[:, blks(j), :],
                                  misc[:].rearrange("p (t d) -> p t d", t=TB), ALU.add).then_inc(S["end_chain"], 1)
            if s == 6:
                wait(dve, S["end_chain"], 3 * j + 1)
                norm_stats(TB, rows_of(j), S["end_chain"])
            if s == 7:
                norm_var(TB, S["end_chain"], 3 * j + 1, S["end_var"])
            if s == 9:
                wait(dve, S["xnext_written"], 16 * j)
                norm_apply(TB, rows_of(j), xnext, S["end_rstd"], j + 1, S["xnext_made"])

        def a_iteration(k, agg, mid, run_ffn, end):
            L, S = LA, SA
            for s in range(STEPS):
                if isinstance(k, int) and k == 0:
                    if s % Y_BLOCKS == 4 and s // Y_BLOCKS + 1 < Y_PIECES:
                        y_low(s // Y_BLOCKS + 1)
                    if s < 30 and 2 <= s % 10 < 7:
                        input_stats(s // 10 + 1, s % 10 - 2)
                    if s < 30 and s % 10 == 7:
                        input_var(s // 10 + 1)
                    if s % 10 < 5 and s < NB:
                        input_norm(s // 10, s % 10)
                if isinstance(k, int) and k == 1 and 24 <= s < 24 + LA.experts:
                    if s == 24:
                        dve.wait_ge(consts_set, 1)
                        dve.wait_ge(small_landed, 16 * 7)
                        dve.wait_ge(up_landed, 32)
                    raw, at = up_weights(s - 24)
                    dve.wait_ge(up_high, s - 24 + 1)
                    split_low(dve, w1l[:, at], raw, w1h[:, at]).then_inc(up_split, 1)
                if agg and s < NB:
                    l = s // LB
                    if s % LB == 0:
                        wait(dve, ring_landed[in_slot(k, l)], in_count(k, l))
                    wait(dve, s_made, k * NB + s + 1)
                    wait(dve, S["agg_blocks"], k * NB + s + 1 - M_BUFS)
                    wait(dve, abs_made, k * NB + s + 1 - M_BUFS)
                    dve.tensor_tensor(m[:, s % M_BUFS, :], sbank[s % 2][:],
                                      ring[:, in_slot(k, l), (s % LB) * CW:(s % LB + 1) * CW], ALU.mult).then_inc(m_made, 1)
                if 3 <= s < NB + 2 and adds_on_vector(k, s - 2):
                    add_abs(dve, k, s - 2)
                edges = agg and not (isinstance(k, int) and k < DEFER)
                if edges and s % LB == 2 and s < NB:
                    i = s // LB
                    wait(dve, late_landed[i % 2], 32 * ((k - DEFER) * (XPER // 2) + i // 2 + 1))
                    if i == 0:
                        wait(dve, redge_chain, 3 * (k - DEFER) + 1)
                    dve.tensor_tensor_reduce(late[:, i % 2, 0, :], late[:, i % 2, 0, :], late[:, i % 2, 1, :],
                                             1.0, 0.0, ALU.mult, ALU.add, xpart[:, i:i + 1]).then_inc(late_read, 1)
                if edges and 1 <= s <= NB:
                    b = s - 1
                    l = b // LB
                    piece = slice((b % LB) * CW, (b % LB + 1) * CW)
                    if b % LB == 0:
                        wait(dve, ring_landed[2 + l % 2], in_count(k, l))
                    if b == 0:
                        wait(dve, redge_chain, 3 * (k - DEFER) + 1)
                    wait(dve, edges_read, (k - DEFER) * NB + b - 1)
                    dve.tensor_tensor_reduce(junk[:, b % 2, :], ring[:, l % 2, piece], ring[:, 2 + l % 2, piece],
                                             1.0, 0.0, ALU.mult, ALU.add, rpart[:, b:b + 1]).then_inc(edges_read, 1)
                if edges and s == NB + 1:
                    wait(dve, edges_read, (k - DEFER + 1) * NB)
                    wait(dve, redge_chain, 3 * (k - DEFER) + 1)
                    dve.tensor_tensor(redge[:], redge[:], rpart[:], ALU.add).then_inc(redge_chain, 1)
                    wait(dve, late_read, (k - DEFER + 1) * XPER)
                    some = redge[:, bass.ds((k - DEFER) * XB, XB)]
                    for c in range(DEFER):
                        wait(dve, redge_chain, 3 * (k - DEFER) + 2 + c)
                        dve.tensor_tensor(some, some, xpart[:, c * XB:(c + 1) * XB], ALU.add).then_inc(redge_chain, 1)
                if mid and s == 2:
                    j = k - 1
                    wait(dve, rowsum_made, j + 1)
                    dve.tensor_scalar(rl[:], misc[:, 0:TB], L1_EPS, None, ALU.max).then_inc(rl_chain, 1)
                    wait(dve, rl_chain, 3 * j + 1)
                    dve.reciprocal(rinv[:], rl[:]).then_inc(rl_chain, 1)
                    wait(dve, rl_chain, 3 * j + 2)
                    dve.tensor_scalar(rinv[:], rinv[:], 1.0 - ALPHA, None, ALU.mult).then_inc(rl_chain, 1)
                if end:
                    a_end(k, s)
                if mid and s == L.at("residual", k):
                    j = k - 1
                    wait(dve, h0_landed, 16 * (j + 1))
                    dve.scalar_tensor_tensor(xres[:, blks(j), :], aux[:], ALPHA, xres[:, blks(j), :], ALU.mult, ALU.add
                                             ).then_inc(S["mid_chain"], 1)
                    wait(dve, S["mid_chain"], 4 * j + 1)
                    wait(dve, rl_chain, 3 * j + 3)
                    wait(dve, S["agg_turned"], j + 1)
                    for t in range(TB):
                        row = xres[:, bass.ds(j * TB + t, 1), :].rearrange("p o d -> p (o d)")
                        last = dve.scalar_tensor_tensor(row, misc[:, t * P:(t + 1) * P], rinv[:, t:t + 1], row,
                                                        ALU.mult, ALU.add)
                    last.then_inc(S["mid_chain"], 1)
                if mid and s == L.at("stats", k):
                    wait(dve, S["mid_chain"], 4 * (k - 1) + 2)
                    norm_stats(0, rows_of(k - 1), S["mid_chain"])
                if mid and s == L.at("var", k):
                    norm_var(0, S["mid_chain"], 4 * (k - 1) + 2, S["mid_var"])
                if mid and s == L.at("norm", k):
                    j = k - 1
                    wait(dve, S["xnc_turned"], j)
                    norm_apply(0, rows_of(j), xnc, S["mid_rstd"], j + 1, S["xnc_made"])
                if run_ffn and s in L.add_step:
                    add_expert(L, S, k - 2, L.add_step.index(s), b2)
                if mid:
                    router_parts(L, S, s, k, k - 1, False)

        pipeline(dve, a_iteration, CH + 2)

        def z_iteration(k, agg, mid, run_ffn, end):
            L, S = LZ, SZ
            for s in range(STEPS):
                if isinstance(k, int) and k == 0 and s < NB and s % TB == 0 and s // TB % 2 == 0:
                    norm_chunk_low(dve, s // TB, xn_low)
                if agg and s < NB:
                    l = s // LB
                    if s % LB == 0:
                        wait(dve, ring2_landed[l % 5], 16 * (k * (LOADS // 5) + l // 5 + 1))
                    wait(dve, adj_high, k * NB + s + 1)
                    split_low(dve, adj_part(1, s), ring[:, l % 5, (s % LB) * CW:(s % LB + 1) * CW],
                              adj_part(0, s)).then_inc(adj_low, 1)
                if isinstance(k, int) and k == 0:
                    a_end(CH + 2, s)
                if run_ffn and lows_on_vector(k):
                    hidden_low(dve, k, s)
                if end and s == L.at("last_add", k):
                    add_expert(L, S, k - 3, L.experts - 1, b2z)
                if end and s == L.at("close", k):
                    j = k - 3
                    wait(dve, S["ffn_turned"], j + 1)
                    wait(dve, S["xnext_written"], 16 * j)
                    dve.tensor_tensor(xnext[:], xres[:, blks(j), :], misc[:].rearrange("p (t d) -> p t d", t=TB),
                                      ALU.add).then_inc(S["xnext_made"], 1)
                if mid and s == L.at("bias", k):
                    xs = xres[:, blks(k - 1), :]
                    if isinstance(k, int) and k == 1:
                        dve.wait_ge(graph_weights_landed, 48)
                    dve.tensor_tensor(xs, xs, wbias.unsqueeze(1).to_broadcast([P, TB, D]), ALU.add
                                      ).then_inc(S["mid_chain"], 1)
                if mid and s == L.at("edge", k):
                    j = k - 1
                    wait(dve, S["mid_chain"], 5 * j + 1)
                    for t in range(TB):
                        row = xres[:, bass.ds(j * TB + t, 1), :].rearrange("p o d -> p (o d)")
                        last = dve.scalar_tensor_tensor(row, wedge, redge[:, bass.ds(j * TB + t, 1)], row,
                                                        ALU.mult, ALU.add)
                    last.then_inc(S["mid_chain"], 1)
                if mid and s == L.at("residual", k):
                    j = k - 1
                    xs = xres[:, blks(j), :]
                    wait(dve, S["mid_chain"], 5 * j + 2)
                    wait(dve, S["agg_turned"], j + 1)
                    dve.tensor_tensor(xs, xs, misc[:].rearrange("p (t d) -> p t d", t=TB), ALU.add
                                      ).then_inc(S["mid_chain"], 1)
                if mid and s == L.at("stats", k):
                    wait(dve, S["mid_chain"], 5 * (k - 1) + 3)
                    norm_stats(0, rows_of(k - 1), S["mid_chain"])
                if mid and s == L.at("var", k):
                    norm_var(0, S["mid_chain"], 5 * (k - 1) + 3, S["mid_var"])
                if mid and s == L.at("norm", k):
                    j = k - 1
                    wait(dve, S["xnc_turned"], j)
                    norm_apply(0, rows_of(j), xnc, S["mid_rstd"], j + 1, S["xnc_made"])
                if run_ffn and s in L.add_step:
                    add_expert(L, S, k - 2, L.add_step.index(s), b2z)
                if mid:
                    router_parts(L, S, s, k, k - 1, True)

        pipeline(dve, z_iteration)

    @block.gpsimd
    def _(pool):
        pool.memset(mhalf[:], -0.5)
        pool.memset(euler[:], float(np.e))
        pool.memset(ones[:], 1.0)
        pool.iota(prio[:], [[0, TB], [-1, E]], base=E, channel_multiplier=0, allow_small_or_imprecise_dtypes=True)
        pool.memset(ident[:], 0.0).then_inc(ident_zeroed, 1)
        pool.wait_ge(ident_zeroed, 1)
        pool.affine_select(out=ident[:], in_=ident[:], compare_op=ALU.not_equal, fill=1.0, base=0,
                           pattern=[[-1, P]], channel_multiplier=1).then_inc(consts_set, 1)

        def input_power(i):
            pool.wait_ge(setup_chain, 3 * i + 3)
            piece = slice(i * 10, i * 10 + 10)
            pool.tensor_tensor(rstd[:, piece], vareps[:, piece], mhalf[:, piece], ALU.pow).then_inc(setup_rstd, 1)

        input_power(0)

        def power(at, var_ready, done, count):
            wait(pool, var_ready, count)
            pool.tensor_tensor(rstd[:, at:at + TB], vareps[:, at:at + TB], mhalf[:, 0:TB], ALU.pow).then_inc(done, 1)

        def exponential(S, j, t):
            if t == 0:
                wait(pool, S["lg_made"], j + 1)
                wait(pool, S["mask_made"], j)
            pool.tensor_tensor(ex[:, t, :], euler[:, t, :], lg[:, t, :], ALU.pow).then_inc(S["exp_made"], 1)

        def a_end(k, s):
            if s == 8:
                power(TB, SA["end_var"], SA["end_rstd"], k - 2)
            if s == 11:
                wait(pool, SA["xnext_made"], k - 2)
                carry(pool, pool_carried)
                pool.dma_start(xn_dram[:, blks(k - 3), :], xnext[:]).then_inc(SA["xnext_written"], 16)

        def a_iteration(k, agg, mid, run_ffn, end):
            for s in range(STEPS):
                if isinstance(k, int) and k == 0 and s % 10 == 7 and s < 30:
                    input_power(s // 10 + 1)
                if agg and 3 <= s < NB + 2 and not adds_on_vector(k, s - 2):
                    add_abs(pool, k, s - 2)
                if end:
                    a_end(k, s)
                for t in range(TB):
                    if mid and s == LA.at("exp", k)[t]:
                        exponential(SA, k - 1, t)
                if mid and s == LA.at("power", k):
                    power(0, SA["mid_var"], SA["mid_rstd"], k)
                if agg and s == 12:
                    wait(pool, SA["mid_chain"], 4 * (k - 1) + 1)
                    carry(pool, pool_carried)
                    pool.dma_start(aux[:], h0_t[:, blks(k), :]).then_inc(h0_landed, 16)

        pipeline(pool, a_iteration, CH + 2)

        def z_iteration(k, agg, mid, run_ffn, end):
            for s in range(STEPS):
                if isinstance(k, int) and k == 0:
                    a_end(CH + 2, s)
                    if s == 13:
                        pool.wait_ge(SA["xnext_written"], 16 * CH)
                        pool.dma_start(xn[:, NB - TB:, :], xn_dram[:, NB - TB:, :]).then_inc(xn_last_landed, 16)
                    if s % TB == 0 and s < NB and s // TB % 2 == 1:
                        norm_chunk_low(pool, s // TB, xn_low_odd)
                if isinstance(k, int) and k == 1 and s == 0:
                    pool.wait_ge(SA["mid_chain"], 4 * CH)
                if isinstance(k, int) and k == 1 and s == 4:
                    pool.wait_ge(up_high, LA.experts + 1)
                    pool.wait_ge(up_landed, 48)
                    split_low(pool, w1l[:, 0:WZ], stage[:, 0:WZ], w1h[:, 0:WZ]).then_inc(up_split, 1)
                if isinstance(k, int) and k == 1 and s == 16:
                    pool.wait_ge(w2_high, 1)
                    pool.wait_ge(weights2_landed, 16)
                    split_low(pool, w2l, stage[:, WZ:2 * WZ], w2h).then_inc(w2_split, 1)
                if mid and s == LZ.at("load_aux", k):
                    wait(pool, aux_turned, k - 1)
                    carry(pool, pool_carried)
                    pool.dma_start(aux[:], xn_dram[:, blks(k - 1), :]).then_inc(aux_landed, 16)
                if end and s == LZ.at("store", k):
                    wait(pool, SZ["xnext_made"], k - 2)
                    carry(pool, pool_carried)
                    pool.dma_start(out[:, blks(k - 3), :], xnext[:]).then_inc(SZ["xnext_written"], 16)
                if run_ffn and not lows_on_vector(k):
                    hidden_low(pool, k, s)
                for t in range(TB):
                    if mid and s == LZ.at("exp", k)[t]:
                        exponential(SZ, k - 1, t)
                if mid and s == LZ.at("power", k):
                    power(0, SZ["mid_var"], SZ["mid_rstd"], k)

        pipeline(pool, z_iteration)
        pool.wait_ge(SZ["xnext_written"], 16 * CH)

    ctx.close()


def kernel(**inputs):
    import concourse.bacc as _bacc
    from concourse import mybir as _mybir
    from concourse.bass_utils import run_bass_kernel_spmd as _run

    a = {k: np.asarray(v) for k, v in inputs.items()}
    pad = CH * CW

    def rows(v):
        full = np.zeros((pad, v.shape[1]), v.dtype)
        full[:N] = v
        return np.ascontiguousarray(full.reshape(NB, P, -1).transpose(1, 0, 2))

    def columns(v):
        full = np.zeros((pad, pad), v.dtype)
        full[:N, :N] = v
        return np.ascontiguousarray(full.reshape(NB, P, CH, CW).transpose(2, 1, 0, 3).reshape(CH, P, NB * CW))

    y_pad = np.zeros((P // 4, pad), a["L0_gnn_y"].dtype)
    y_pad[:CLS, :N] = a["L0_gnn_y"].T

    def per_partition(*parts):
        return np.ascontiguousarray(np.concatenate([v.reshape(-1, P) for v in parts]).T)

    arrays = {
        "x_t": rows(a["x"]),
        "adj_in": columns(a["adj"].T),
        "adj_out": columns(a["adj"]),
        "h0_t": rows(a["L0_gnn_h0"]),
        "y_t": y_pad,
        "wr0": a["L0_ffn_Wr"],
        "w1s": a["L0_ffn_W1s"],
        "b1_0": per_partition(a["L0_ffn_b1s"], a["L0_ffn_b1p"]),
        "w2s": a["L0_ffn_W2s"],
        "b2_0": per_partition(a["L0_ffn_b2s"], a["L0_ffn_b2p"]),
        "w1p": a["L0_ffn_W1p"],
        "w2p": a["L0_ffn_W2p"],
        "wg": a["L1_gnn_weight"],
        "wg_bias": a["L1_gnn_bias"].reshape(1, -1),
        "gate_w": a["L1_ffn_gate_w"],
        "gate_b": np.tile(a["L1_ffn_gate_b"], TB).reshape(1, -1),
        "w1_1": a["L1_ffn_W1"],
        "b1_1": per_partition(a["L1_ffn_b1"]),
        "w2_1": a["L1_ffn_W2"],
        "b2_1": per_partition(a["L1_ffn_b2"]),
    }
    nc = _bacc.Bacc("TRN2", target_bir_lowering=False, num_devices=1, dynamic_dma_scratch_size=4096)
    args, feed = [], {}
    for name, v in arrays.items():
        feed[f"in_{name}"] = np.ascontiguousarray(v)
        args.append(nc.dram_tensor(f"in_{name}", v.shape, _mybir.dt.from_np(v.dtype), kind="ExternalInput").ap())
    args.append(nc.dram_tensor("out_x", [P, NB, D], _mybir.dt.float32, kind="ExternalOutput").ap())
    bass_two_layer_gnn_moe_kernel(nc, *args)
    r = _run(nc, [feed], core_ids=[0])
    got = r.results[0]["out_x"]
    return np.ascontiguousarray(got.transpose(1, 0, 2).reshape(pad, D)[:N])
```
